# Optimizing a Trainium2 kernel written in Bass

```python
import numpy as np
import jax
import jax.numpy as jnp

def _softmax(x, axis=-1):
    return jax.nn.softmax(x, axis=axis)

def _gelu(x):
    return jax.nn.gelu(x, approximate=True)

def _silu(x):
    return jax.nn.silu(x)

def _sigmoid(x):
    return jax.nn.sigmoid(x)

def _layernorm(x, axis=-1, eps=1e-05):
    m = jnp.mean(x, axis=axis, keepdims=True)
    v = jnp.var(x, axis=axis, keepdims=True)
    return (x - m) / jnp.sqrt(v + eps)

def _scatter_add(tgt, idx, src, axis=0):
    return tgt.at[idx].add(src)

def _segment_sum(src, seg, n):
    return jax.ops.segment_sum(src, seg, n)
kernel_name = 'mk_gnn_preln_d4_gnn_r8_cc646c'

def setup_inputs(seed: int=0):
    np.random.seed(seed)
    _w = jnp.asarray

    def _rec_inputs():
        import jax
        import jax.numpy as jnp
        _gk = jax.random.key(seed)
        x = -0.0003713 + 1 * jax.random.normal(jax.random.fold_in(_gk, 1), (6250, 128), jnp.float32)
        _s = jax.random.randint(jax.random.fold_in(_gk, 2), (100000,), 0, 6250, jnp.int32)
        _d = jax.random.randint(jax.random.fold_in(_gk, 3), (100000,), 0, 6250, jnp.int32)
        _loop = jnp.arange(6250, dtype=jnp.int32)
        src = jnp.concatenate([_s, _d, _loop])
        dst = jnp.concatenate([_d, _s, _loop])
        _o = jnp.argsort(dst, stable=True)
        src = src[_o]
        dst = dst[_o]
        edge_attr_48 = 5.93493e-05 + 1.00006 * jax.random.normal(jax.random.fold_in(_gk, 13), (206250, 48), jnp.float32)
        return (x, src, dst, edge_attr_48)
    x, src, dst, edge_attr_48 = _rec_inputs()

    def _L0_gnn_setup():
        import jax, jax.numpy as jnp
        import numpy as np
        N_NODES = 12500
        N_EDGES = 200000
        D_IN = 128
        D_OUT = 128
        key = jax.random.key(seed)
        k1, k2, k3, k4, k5 = jax.random.split(key, 5)
        feat = jax.random.normal(k1, (N_NODES, D_IN), dtype=jnp.float32)
        src = jax.random.randint(k2, (N_EDGES,), 0, N_NODES, dtype=jnp.int32)
        dst = jax.random.randint(k3, (N_EDGES,), 0, N_NODES, dtype=jnp.int32)
        w_self = jax.random.normal(k4, (D_IN, D_OUT), dtype=jnp.float32) / np.sqrt(D_IN).astype(np.float32)
        w_neigh = jax.random.normal(k5, (D_IN, D_OUT), dtype=jnp.float32) / np.sqrt(D_IN).astype(np.float32)
        b_neigh = jnp.zeros((D_OUT,), dtype=jnp.float32)
        return {'feat': feat, 'w_self': w_self, 'w_neigh': w_neigh, 'b_neigh': b_neigh, 'src': src, 'dst': dst}
    _L0_gnn_all = _L0_gnn_setup()
    _L0_gnn_in = {k: v for k, v in _L0_gnn_all.items() if k in ('w_self', 'w_neigh', 'b_neigh')}
    del _L0_gnn_all

    def _L1_gnn_setup():
        import jax, jax.numpy as jnp
        import numpy as np
        N = 6250
        E = 75000
        D = 128
        G = 8
        EPS = 1e-05
        key = jax.random.key(seed)
        ks = jax.random.split(key, 8)
        x = jax.random.normal(ks[0], (N, D), dtype=jnp.float32)
        edge_index = jax.random.randint(ks[1], (2, E), 0, N)
        batch = jnp.sort(jax.random.randint(ks[2], (N,), 0, G))
        s = 1.0 / np.sqrt(D)
        Wl = jax.random.normal(ks[3], (D, D), dtype=jnp.float32) * s
        bl = jax.random.normal(ks[4], (D,), dtype=jnp.float32) * s
        Wr = jax.random.normal(ks[5], (D, D), dtype=jnp.float32) * s
        return {'x': x, 'edge_index': edge_index, 'batch': batch, 'num_graphs': G, 'Wl': Wl, 'bl': bl, 'Wr': Wr, 'gn_weight': jnp.ones((D,), jnp.float32), 'gn_bias': jnp.zeros((D,), jnp.float32), 'mean_scale': jnp.ones((D,), jnp.float32)}
    _L1_gnn_all = _L1_gnn_setup()
    _L1_gnn_in = {k: v for k, v in _L1_gnn_all.items() if k in ('Wl', 'bl', 'Wr', 'gn_weight', 'gn_bias', 'mean_scale')}
    del _L1_gnn_all

    def _L2_gnn_setup():
        import jax, jax.numpy as jnp
        import numpy as np
        N, E, D = (6250, 78125, 128)
        L, H, C = (3, 4, 32)
        NEG_SLOPE = 0.2

        def _gat_layer(x, src, dst, W_i, a_src_i, a_dst_i, b_i):
            n = x.shape[0]
            h = (x @ W_i).reshape(n, H, C)
            es = jnp.einsum('nhc,hc->nh', h, a_src_i)
            ed = jnp.einsum('nhc,hc->nh', h, a_dst_i)
            e = es[src] + ed[dst]
            e = jnp.where(e > 0, e, NEG_SLOPE * e)
            m = jax.ops.segment_max(e, dst, num_segments=n)
            p = jnp.exp(e - m[dst])
            denom = jax.ops.segment_sum(p, dst, num_segments=n)
            alpha = p / denom[dst]
            msg = alpha[:, :, None] * h[src]
            out = jax.ops.segment_sum(msg, dst, num_segments=n)
            return out.reshape(n, H * C) + b_i
        key = jax.random.key(seed)
        ks = jax.random.split(key, 6)
        x = jax.random.normal(ks[0], (N, D), dtype=jnp.float32)
        edge_index = jax.random.randint(ks[1], (2, E), 0, N, dtype=jnp.int32)
        W = jax.random.normal(ks[2], (L, D, H * C), dtype=jnp.float32) * 0.1
        att_src = jax.random.normal(ks[3], (L, H, C), dtype=jnp.float32) * 0.1
        att_dst = jax.random.normal(ks[4], (L, H, C), dtype=jnp.float32) * 0.1
        bias = jnp.zeros((L, H * C), dtype=jnp.float32)
        return {'x': x, 'edge_index': edge_index, 'W': W, 'att_src': att_src, 'att_dst': att_dst, 'bias': bias}
    _L2_gnn_all = _L2_gnn_setup()
    _L2_gnn_in = {k: v for k, v in _L2_gnn_all.items() if k in ('W', 'att_src', 'att_dst', 'bias')}
    del _L2_gnn_all

    def _L3_gnn_setup():
        import jax, jax.numpy as jnp
        import numpy as np
        N, E, NODE_D, EDGE_D, GLOB_D, HID, B = (12500, 200000, 128, 48, 16, 256, 64)
        key = jax.random.key(seed)
        ks = jax.random.split(key, 9)
        x = jax.random.normal(ks[0], (N, NODE_D), dtype=jnp.float32)
        edge_index = jax.random.randint(ks[1], (2, E), 0, N, dtype=jnp.int32)
        edge_attr = jax.random.normal(ks[2], (E, EDGE_D), dtype=jnp.float32)
        u = jax.random.normal(ks[3], (B, GLOB_D), dtype=jnp.float32)
        batch = jnp.sort(jax.random.randint(ks[4], (N,), 0, B, dtype=jnp.int32))
        in_dim = NODE_D + 3 * EDGE_D + GLOB_D
        s1 = 1.0 / np.sqrt(in_dim)
        s2 = 1.0 / np.sqrt(HID)
        W1 = jax.random.uniform(ks[5], (in_dim, HID), jnp.float32, -s1, s1)
        b1 = jax.random.uniform(ks[6], (HID,), jnp.float32, -s1, s1)
        W2 = jax.random.uniform(ks[7], (HID, NODE_D), jnp.float32, -s2, s2)
        b2 = jax.random.uniform(ks[8], (NODE_D,), jnp.float32, -s2, s2)
        return {'x': x, 'edge_index': edge_index, 'edge_attr': edge_attr, 'u': u, 'batch': batch, 'W1': W1, 'b1': b1, 'W2': W2, 'b2': b2}
    _L3_gnn_all = _L3_gnn_setup()
    _L3_gnn_in = {k: v for k, v in _L3_gnn_all.items() if k in ('u', 'W1', 'b1', 'W2', 'b2')}
    del _L3_gnn_all
    return {'x': x, 'src': src, 'dst': dst, 'edge_attr_48': edge_attr_48, 'L0_gnn_w_self': _L0_gnn_in['w_self'], 'L0_gnn_w_neigh': _L0_gnn_in['w_neigh'], 'L0_gnn_b_neigh': _L0_gnn_in['b_neigh'], 'L1_gnn_Wl': _L1_gnn_in['Wl'], 'L1_gnn_bl': _L1_gnn_in['bl'], 'L1_gnn_Wr': _L1_gnn_in['Wr'], 'L1_gnn_gn_weight': _L1_gnn_in['gn_weight'], 'L1_gnn_gn_bias': _L1_gnn_in['gn_bias'], 'L1_gnn_mean_scale': _L1_gnn_in['mean_scale'], 'L2_gnn_W': _L2_gnn_in['W'], 'L2_gnn_att_src': _L2_gnn_in['att_src'], 'L2_gnn_att_dst': _L2_gnn_in['att_dst'], 'L2_gnn_bias': _L2_gnn_in['bias'], 'L3_gnn_u': _L3_gnn_in['u'], 'L3_gnn_W1': _L3_gnn_in['W1'], 'L3_gnn_b1': _L3_gnn_in['b1'], 'L3_gnn_W2': _L3_gnn_in['W2'], 'L3_gnn_b2': _L3_gnn_in['b2']}

def reference(x, src, dst, edge_attr_48, L0_gnn_w_self, L0_gnn_w_neigh, L0_gnn_b_neigh, L1_gnn_Wl, L1_gnn_bl, L1_gnn_Wr, L1_gnn_gn_weight, L1_gnn_gn_bias, L1_gnn_mean_scale, L2_gnn_W, L2_gnn_att_src, L2_gnn_att_dst, L2_gnn_bias, L3_gnn_u, L3_gnn_W1, L3_gnn_b1, L3_gnn_W2, L3_gnn_b2):
    import jax
    import jax.numpy as jnp

    def _L0_gnn_ref(feat, w_self, w_neigh, b_neigh, src, dst):
        import jax, jax.numpy as jnp
        import numpy as np
        N_NODES = 12500
        N_EDGES = 200000
        D_IN = 128
        D_OUT = 128
        n = feat.shape[0]
        msg_sum = jax.ops.segment_sum(feat[src], dst, num_segments=n)
        deg = jax.ops.segment_sum(jnp.ones_like(dst, dtype=feat.dtype), dst, num_segments=n)
        h_neigh = msg_sum / jnp.maximum(deg, 1.0)[:, None]
        return feat @ w_self + h_neigh @ w_neigh + b_neigh

    def _L1_gnn_ref(x, edge_index, batch, num_graphs, Wl, bl, Wr, gn_weight, gn_bias, mean_scale):
        import jax, jax.numpy as jnp
        import numpy as np
        N = 6250
        E = 75000
        D = 128
        G = 8
        EPS = 1e-05
        n = x.shape[0]
        src, dst = (edge_index[0], edge_index[1])
        ones_e = jnp.ones(src.shape[0], dtype=x.dtype)
        deg = jax.ops.segment_sum(ones_e, dst, num_segments=n)
        agg = jax.ops.segment_sum(x[src], dst, num_segments=n)
        agg = agg / jnp.maximum(deg, 1.0)[:, None]
        f = agg @ Wl.T + bl + x @ Wr.T
        f = jax.nn.gelu(f, approximate=False)
        ones_n = jnp.ones(n, dtype=x.dtype)
        cnt = jax.ops.segment_sum(ones_n, batch, num_segments=num_graphs)[:, None]
        mean = jax.ops.segment_sum(f, batch, num_segments=num_graphs) / cnt
        out = f - mean_scale * mean[batch]
        var = jax.ops.segment_sum(out * out, batch, num_segments=num_graphs) / cnt
        out = out / jnp.sqrt(var[batch] + EPS) * gn_weight + gn_bias
        return out + x

    def _L2_gnn_ref(x, edge_index, W, att_src, att_dst, bias):
        import jax, jax.numpy as jnp
        import numpy as np
        N, E, D = (6250, 78125, 128)
        L, H, C = (3, 4, 32)
        NEG_SLOPE = 0.2

        def _gat_layer(x, src, dst, W_i, a_src_i, a_dst_i, b_i):
            n = x.shape[0]
            h = (x @ W_i).reshape(n, H, C)
            es = jnp.einsum('nhc,hc->nh', h, a_src_i)
            ed = jnp.einsum('nhc,hc->nh', h, a_dst_i)
            e = es[src] + ed[dst]
            e = jnp.where(e > 0, e, NEG_SLOPE * e)
            m = jax.ops.segment_max(e, dst, num_segments=n)
            p = jnp.exp(e - m[dst])
            denom = jax.ops.segment_sum(p, dst, num_segments=n)
            alpha = p / denom[dst]
            msg = alpha[:, :, None] * h[src]
            out = jax.ops.segment_sum(msg, dst, num_segments=n)
            return out.reshape(n, H * C) + b_i
        n = x.shape[0]
        loops = jnp.arange(n, dtype=edge_index.dtype)
        src = jnp.concatenate([edge_index[0], loops])
        dst = jnp.concatenate([edge_index[1], loops])
        for i in range(L):
            x = jax.nn.elu(_gat_layer(x, src, dst, W[i], att_src[i], att_dst[i], bias[i]))
        return x

    def _L3_gnn_ref(x, edge_index, edge_attr, u, batch, W1, b1, W2, b2):
        import jax, jax.numpy as jnp
        import numpy as np
        N, E, NODE_D, EDGE_D, GLOB_D, HID, B = (12500, 200000, 128, 48, 16, 256, 64)
        col = edge_index[1]
        n = x.shape[0]
        out1 = jax.ops.segment_sum(edge_attr, col, num_segments=n)
        mx = jax.ops.segment_max(edge_attr, col, num_segments=n)
        cnt = jax.ops.segment_sum(jnp.ones((edge_attr.shape[0],), edge_attr.dtype), col, num_segments=n)
        has = (cnt > 0)[:, None]
        out2 = jnp.where(has, mx, 0.0)
        out3 = out1 / jnp.maximum(cnt, 1.0)[:, None]
        feat = jnp.concatenate([x, out1, out2, out3, u[batch]], axis=1)
        h = jax.nn.relu(feat @ W1 + b1)
        out = h @ W2 + b2
        return out + x
    edge_index = jnp.stack([src, dst])
    batch0 = jnp.zeros((6250,), jnp.int32)
    h = jnp.maximum(_layernorm(x, axis=-1), 0.0)
    x = x + _L0_gnn_ref(h, L0_gnn_w_self, L0_gnn_w_neigh, L0_gnn_b_neigh, src, dst)
    h = jnp.maximum(_layernorm(x, axis=-1), 0.0)
    x = x + _L1_gnn_ref(h, edge_index, batch0, 8, L1_gnn_Wl, L1_gnn_bl, L1_gnn_Wr, L1_gnn_gn_weight, L1_gnn_gn_bias, L1_gnn_mean_scale)
    h = jnp.maximum(_layernorm(x, axis=-1), 0.0)
    x = x + _L2_gnn_ref(h, edge_index, L2_gnn_W, L2_gnn_att_src, L2_gnn_att_dst, L2_gnn_bias)
    h = jnp.maximum(_layernorm(x, axis=-1), 0.0)
    x = x + _L3_gnn_ref(h, edge_index, edge_attr_48, L3_gnn_u, batch0, L3_gnn_W1, L3_gnn_b1, L3_gnn_W2, L3_gnn_b2)
    return x

_drawn_inputs = setup_inputs


def setup_inputs(seed=0):
    import zlib

    import numpy as np

    out = dict(_drawn_inputs(seed))
    spreads = {'L0_gnn_b_neigh': (0.0, 0.1),
     'L1_gnn_gn_weight': (1.0, 0.2),
     'L1_gnn_gn_bias': (0.0, 0.1),
     'L1_gnn_mean_scale': (1.0, 0.2),
     'L2_gnn_bias': (0.0, 0.1)}
    factors = {'L2_gnn_att_src': 3.822,
     'L2_gnn_att_dst': 8.0,
     'L3_gnn_u': 2.984,
     'L3_gnn_b1': 8.0,
     'L3_gnn_b2': 4.444}
    for name, (base, spread) in spreads.items():
        noise = np.random.default_rng([zlib.crc32(name.encode()), seed]).standard_normal(out[name].shape)
        drawn = base * np.exp(spread * noise) if base else spread * noise
        out[name] = jnp.asarray(drawn.astype(out[name].dtype))
    for name, factor in factors.items():
        out[name] = (out[name] * factor).astype(out[name].dtype)
    return out
```

```python
from collections import namedtuple
from contextlib import ExitStack

import concourse.bass as bass
from concourse import mybir

P = 128
D = 128
HEADS = 4
HC = D // HEADS
HW = HC + 1
AW = HEADS * HW
ROW = AW + HEADS
LAYERS = 3
EA = 48
UD = 16
HID = 256
ROUND = 8
GROUP = 32
RG = GROUP // ROUND
TG = 7
SD_W = 2 * P + 4
EPS = 1e-5
SLOPE = 0.2
PARTS = 3
LEAD = 4
FAR = -1.0e30
EDGE_FAR = -3.0e38

F32 = mybir.dt.float32
I32 = mybir.dt.int32
BF16 = mybir.dt.bfloat16
ALU = mybir.AluOpType
ACT = mybir.ActivationFunctionType
AX = mybir.AxisListType
DVE_E = mybir.EngineType.DVE
PE_E = mybir.EngineType.PE
BOUNDED = "tile indices are clamped to the last tile when the table is made"


Geometry = namedtuple("Geometry", "nodes edges tiles chunks slots blocks rows groups")


def geometry(nodes, edges):
    tiles = -(-nodes // (P * TG)) * TG
    chunks = -(-edges // P)
    slots = -(-(chunks + tiles - 1) // (2 * GROUP)) * 2 * GROUP
    blocks = slots // P if slots % P == 0 else slots // P + 1
    return Geometry(nodes=nodes, edges=edges, tiles=tiles, chunks=chunks, slots=slots,
                    blocks=blocks, rows=blocks * P, groups=slots // GROUP)


def build_graph_network(nc, g, a, out):
    NT, NS, NB, NR, NG = g.tiles, g.slots, g.blocks, g.rows, g.groups
    NTG = NT // TG
    FREE_BANKS = 4
    FREE = 1

    table = nc.dram_tensor("row_table", [NT * P, ROW], F32).ap()
    slot_first = nc.dram_tensor("slot_first", [NR, 1], F32).ap()
    change_rows = nc.dram_tensor("change_rows", [NR, P + 1], F32).ap()
    dst_rows = nc.dram_tensor("dst_rows", [NR + GROUP, P], BF16).ap()
    slot_masks = nc.dram_tensor("slot_masks", [3, NR + GROUP], F32).ap()
    new_segment = nc.dram_tensor("new_segment", [NR * P], F32).ap()
    same_segment = nc.dram_tensor("same_segment", [NR * P], F32).ap()
    edge_stats = nc.dram_tensor("edge_stats", [NR * P, 2 * EA], F32).ap()

    with ExitStack() as ctx:
        def sb(name, shape, dt=F32):
            return ctx.enter_context(nc.sbuf_tensor(name, shape, dt))

        def sem(name):
            return ctx.enter_context(nc.semaphore(name))

        def sems(stage, names):
            return namedtuple(stage, names)(*[sem(f"{stage}_{n}") for n in names.split()])

        ctx.enter_context(nc.allow_non_contiguous_dma(reason="tables of indices, a few KB"))
        bank = ctx.enter_context(nc.psum_tensor("bank", [P, 8, 512], F32))

        X = sb("X", [P, NT, D])
        H = sb("H", [P, NT, ROW])
        acc = sb("acc", [P, NT * ROW])
        dst_local = sb("dst_local", [P, NR + 2 * GROUP])
        src_of = sb("src_of", [P, NR + 2 * GROUP])
        last_edge = sb("last_edge", [P, NR + 2 * GROUP], BF16)
        offsets = sb("offsets", [64, NR + 2 * GROUP], I32)
        dst_score = sb("dst_score", [P, NT * HEADS])
        dst_parts = sb("dst_parts", [P, NT * PARTS * HEADS], BF16)
        gathered = sb("gathered", [P, 2 * GROUP, ROW])
        pick = sb("pick", [P, GROUP, P])
        staged_idx = sb("staged_idx", [P, 2 * GROUP], I32)
        node_stat = sb("node_stat", [P, 6, NT])
        degree, inv_degree, has_edge, no_edge_far, real_node, rows_before = (
            node_stat[:, k, :] for k in range(6))
        last_row = sb("last_row", [P, NT], I32)

        ident = sb("ident", [P, P])
        col_index = sb("col_index", [P, P])
        tri = sb("tri", [P, P])
        tri_strict = sb("tri_strict", [P, P])
        ones = sb("ones", [P, P])
        part_index = sb("part_index", [P, 1])
        w_self = sb("w_self", [D, D])
        w_neigh = sb("w_neigh", [D, D])
        w_l = sb("w_l", [D, D])
        w_r = sb("w_r", [D, D])
        w_att = sb("w_att", [D, LAYERS, D + 2 * HEADS])
        att_vec = sb("att_vec", [D, LAYERS, 2 * HEADS])
        w1 = sb("w1", [P, 4, HID])
        w2 = sb("w2", [P, 2, D])
        bias_row = sb("bias_row", [1, 3, D])
        att_bias = sb("att_bias", [P, LAYERS, D])
        norm_par = sb("norm_par", [P, 3, D])
        u0 = sb("u0", [UD, 1])
        b1 = sb("b1", [P, 2])

        WEIGHTS = 2 * LAYERS * HEADS + 18 + LAYERS

        GW = TG * D
        scratch_mem = sb("scratch", [P, 6 * GW + 3 * TG * EA])

        def over(start, parts, *shape):
            size = 1
            for n in shape:
                size *= n
            v = scratch_mem[0:parts, start:start + size]
            return v.rearrange("p (a b) -> p a b", a=shape[0]) if len(shape) == 2 else v

        xc, sq, xn, tr_a, tr_b = (over(n * GW, P, TG, D) for n in range(5))
        tr_c = over(5 * GW, EA, TG, P)
        cat = over(6 * GW, P, TG, 3 * EA)
        small = sb("small", [P, 4, TG])
        selfs = sb("selfs", [P, 6, TG, HEADS])
        ea_in = scratch_mem[:, 0:2 * ROUND * EA].rearrange("p (b c w) -> p b c w", b=2, c=ROUND)
        ea_flag = over(2 * ROUND * EA, EA, 2, ROUND * P)
        ea_scan = over(2 * ROUND * (EA + P), EA, 1024)
        ea_out = over(2 * ROUND * (EA + P) + 1024, P, 2, ROUND * EA)
        start_flag = over(0, GROUP, 2, HEADS * P)
        end_flag = over(1024, GROUP, 2, HEADS * P)
        seg_f = over(2048, GROUP, 512)
        seg_m = over(2560, GROUP, 512)
        grp_sb = over(3072, GROUP, 512)
        raw, score, prob = (over(3584 + n * P, P, HEADS, GROUP) for n in range(3))
        masks = sb("masks", [HEADS, 2, 3, GROUP + 1])
        carry_f = sb("carry_f", [HEADS, GROUP + 1])
        carry_b = sb("carry_b", [HEADS, GROUP + 1])
        cross = sb("cross", [HEADS, 2, GROUP])
        pick_t = scratch_mem[:, 3968:3968 + GROUP * P // 2].bitcast(BF16).rearrange("p (k e) -> p k e", k=GROUP)
        pick_dist = sb("pick_dist", [P, ROUND, P], BF16)
        log_scale = sb("log_scale", [1, HEADS])
        old_scale = sb("old_scale", [P, HEADS])

        acc_f = acc[:, :]
        sd_row = acc_f[:, 0:NB * SD_W].bitcast(I32).rearrange("p (k c) -> p k c", k=NB)
        dst_row = acc_f[:, NB * SD_W:NB * (SD_W + P + 1)].rearrange("p (k c) -> p k c", k=NB)
        big = gathered[:, :, :].rearrange("p a b -> p (a b)")

        def part(n):
            return big[:, n * NB * P:(n + 1) * NB * P]

        first_row, scratch = part(0), part(1)
        diag = part(2).rearrange("p (k c) -> p k c", k=NB)
        edge_now, edge_before = (part(n).bitcast(I32).rearrange("p (k c) -> p k c", k=NB) for n in (3, 4))
        h_f = H[:, :, :].rearrange("p a b -> p (a b)")
        src_row = h_f[:, 0:NB * P].rearrange("p (k c) -> p k c", k=NB)
        change = h_f[:, NB * P:NB * (2 * P + 1)].rearrange("p (k c) -> p k c", k=NB)
        is_last = h_f[:, NB * (2 * P + 1):NB * (3 * P + 1)].rearrange("p (k c) -> p k c", k=NB)
        pick_f = pick[:, :, :].rearrange("p a b -> p (a b)")
        flag_a = pick_f[:, 0:NB * P].rearrange("p (k c) -> p k c", k=NB)
        flag_b = pick_f[:, NB * P:2 * NB * P].rearrange("p (k c) -> p k c", k=NB)
        change_keep = pick_f[:, 0:NB * (P + 1)].rearrange("p (k c) -> p k c", k=NB)
        half = NB * (P + 1) + P
        dst_bf = pick_f[:, half:half + NB * P // 2].bitcast(BF16).rearrange("p (k c) -> p k c", k=NB)
        dst_tail = pick_f[0:GROUP, half + NB * P // 2:half + (NB + 1) * P // 2].bitcast(BF16)
        masks_row = big[0:1, 0:3 * (NR + GROUP)].rearrange("p (m n) -> p m n", m=3)
        line_a, line_b, line_c, line_d = (acc[0:1, n * NR:(n + 1) * NR] for n in range(4))
        edge_cmp = part(1).bitcast(I32).rearrange("p (k c) -> p k c", k=NB)
        tile_cols = over(0, P, NB, 33)
        end_cols = sb("end_cols", [P, 2, NB])
        node_stats_in = big[:, 0:NT * 2 * EA].rearrange("p (t w) -> p t w", w=2 * EA)
        hid = pick_f[:, 0:2 * TG * P].rearrange("p (m n) -> p m n", m=2)
        cross_rows = sb("cross_rows", [GROUP, 2 * HEADS])
        iota_nodes = sb("iota_nodes", [P, NT], I32)
        pro = sb("pro", [P, 12, NB])
        (slot_no, chunk_tile, chunk_last, count, before, total, upto, slots_to, chunk_of, first_of, tile_of,
         tmp) = (pro[:, n, :] for n in range(12))
        chunk_idx = sb("chunk_idx", [P, NB], I32)
        int_tmp = sb("int_tmp", [P, NB, 2], I32)
        iota_i = sb("iota_i", [P, P], I32)
        iota_s = sb("iota_s", [P, 1 + NB], I32)

        acc_t = acc[:, :].rearrange("p (t w) -> p t w", w=ROW)
        parts_t = dst_parts[:, :].rearrange("p (t m h) -> p t m h", m=PARTS, h=HEADS)
        score_t = dst_score[:, :].rearrange("p (t h) -> p t h", h=HEADS)
        rows_a = bank[:, 0:4, :].rearrange("p a b -> p (a b)")
        rows_b = bank[:, 4:8, :].rearrange("p a b -> p (a b)")

        pre = sems("pre", "x_loaded weights_loaded tables_loaded zeroed iota const counted prefixed placed spread "
                          "firsts_stored dst_kept dst_stored indexed rows_gathered firsts_gathered split turned_a copied_a turned_b "
                          "copied_b edge_flags flags_stored changes changes_stored w_turned w_copied w_made w_kept "
                          "ends_turned masks_ready masks_stored tail_zeroed")
        dve_tick = sem("vector_tick")
        pe_tick = sem("tensor_tick")
        tick = sem("pool_tick")
        n0 = sems("n0", "var root rows stored")
        n1 = sems("n1", "degrees prefixed scaled turned copied product summed var root rows stored")
        n2 = sems("n2", "scaled turned copied product gelu centred colsum squares colvar var root next turned2 copied2 "
                        "product2 rows stored")
        n3 = sems("n3", "scored weights updated var root next turned copied product rows stored hidden relu "
                        "stats_gathered hid_bias")
        mean = sems("mean", "staged gathered0 gathered1 gathered2 gathered3 picked loaded0 loaded1 turned "
                            "scanned turned_back copied stored0 stored1 summed added")
        att = sems("att", "staged picked rows_loaded turned dst_scored summed added flags0 flags1 "
                          "scored score_rows firsts ends crossed cross_rows maxima max_back shifted prob "
                          "log_scale scale_rows scale weighted used")
        att_gathered = [[sem(f"att{n}_gathered{b}") for b in range(2)] for n in range(LAYERS)]
        mean_gathered = [mean.gathered0, mean.gathered1, mean.gathered2, mean.gathered3]
        mean_loaded = [mean.loaded0, mean.loaded1]
        mean_stored = [mean.stored0, mean.stored1]
        att_flags = [att.flags0, att.flags1]
        RNG = GROUP // ROUND
        ROUNDS = NS // ROUND
        PAIRS = NG // 2
        MEAN_W = D + 1
        QG = GROUP // 4

        block = ctx.enter_context(nc.Block())

        @block.sync
        def _(sp):
            sp.dma_start(X[:, :, :], a["x"].rearrange("(t p) d -> p t d", p=P)).then_inc(pre.x_loaded, 16)
            sp.dma_start(edge_now, a["dst_line"][1:1 + NR * P].rearrange("(k q e) -> q k e", q=P, e=P)
                         ).then_inc(pre.tables_loaded, 16)
            sp.dma_start(edge_before, a["dst_line"][0:NR * P].rearrange("(k q e) -> q k e", q=P, e=P)
                         ).then_inc(pre.tables_loaded, 16)
            sp.wait_ge(pre.zeroed, 1)
            weights = 0
            for n in range(LAYERS):
                for h in range(HEADS):
                    for v, name in enumerate(("att_src", "att_dst")):
                        sp.dma_start(att_vec[h * HC:(h + 1) * HC, n, v * HEADS + h:v * HEADS + h + 1],
                                     a[name][n, h, :].unsqueeze(1)).then_inc(pre.weights_loaded, 16)
                        weights += 1
            for dst, src in ((w_self[:, :], a["w_self"]), (w_neigh[:, :], a["w_neigh"]),
                             (w_l[:, :], a["w_l"]), (w_r[:, :], a["w_r"]),
                             (w_att[:, :, 0:D], a["w_att"].rearrange("l k n -> k l n")),
                             (w1[:, 0, :], a["w1"][0:D, :]),
                             (w1[0:2 * EA, 1, :], a["w1"][D:D + 2 * EA, :]),
                             (w1[0:EA, 2, :], a["w1"][D + 2 * EA:D + 3 * EA, :]),
                             (w1[0:UD, 3, :], a["w1"][D + 3 * EA:D + 3 * EA + UD, :]),
                             (w2[:, :, :], a["w2"].rearrange("(m k) n -> k m n", k=P)),
                             (bias_row[0:1, 0, :], a["b_neigh"].unsqueeze(0)),
                             (bias_row[0:1, 1, :], a["b_l"].unsqueeze(0)),
                             (bias_row[0:1, 2, :], a["b2"].unsqueeze(0)),
                             (u0[:, :], a["u"][0, :].unsqueeze(1)),
                             (b1[:, :], a["b1"].rearrange("(m k) -> k m", k=P)),
                             (norm_par[:, 0, :], a["gn_weight"].unsqueeze(0).to_broadcast([P, D])),
                             (norm_par[:, 1, :], a["gn_bias"].unsqueeze(0).to_broadcast([P, D])),
                             (norm_par[:, 2, :], a["mean_scale"].unsqueeze(0).to_broadcast([P, D]))):
                sp.dma_start(dst, src).then_inc(pre.weights_loaded, 16)
                weights += 1
            for n in range(LAYERS):
                sp.dma_start(att_bias[:, n, :], a["att_bias"][n, :].unsqueeze(0).to_broadcast([P, D])
                             ).then_inc(pre.weights_loaded, 16)
                weights += 1
            assert weights == WEIGHTS
            sp.wait_ge(pre.placed, 1)
            sp.dma_start(slot_first.rearrange("(k q) o -> q (k o)", q=P), before).then_inc(pre.firsts_stored, 16)
            sp.wait_ge(pre.edge_flags, 1)
            sp.dma_start(new_segment.rearrange("(k q e) -> q k e", q=P, e=P), flag_a).then_inc(pre.flags_stored, 16)
            sp.dma_start(same_segment.rearrange("(k q e) -> q k e", q=P, e=P), flag_b).then_inc(pre.flags_stored, 16)
            sp.wait_ge(pre.changes, 1)
            sp.dma_start(change_rows.rearrange("(k q) e -> q k e", q=P), change_keep
                         ).then_inc(pre.changes_stored, 16)
            sp.wait_ge(pre.dst_kept, 1)
            sp.dma_start(dst_rows[0:NR, :].rearrange("(k q) e -> q k e", q=P), dst_bf).then_inc(pre.dst_stored, 16)
            sp.dma_start(dst_rows[NR:NR + GROUP, :], dst_tail).then_inc(pre.dst_stored, 16)
            sp.wait_ge(pre.masks_ready, 1)
            sp.dma_start(slot_masks.unsqueeze(0), masks_row).then_inc(pre.masks_stored, 16)
            with sp.Fori(0, NTG) as i:
                sp.wait_ge(n0.rows, i + 1)
                sp.dma_start(table.rearrange("(t p) w -> p t w", p=P)[:, bass.ds(i * TG, TG), :],
                             H[:, bass.ds(i * TG, TG), :]).then_inc(n0.stored, 16)

            def mean_loads(n):
                with sp.Fori(0, NG) as it:
                    for q in range(RNG):
                        base = n * ROUNDS
                        b = q % 2
                        if q < 2:
                            sp.wait_ge(mean.scanned, base + it * RNG + q + FREE)
                        else:
                            sp.wait_ge(mean.scanned, base + it * RNG + q - 1 + FREE)
                        at = it * (GROUP * P) + q * ROUND * P
                        sp.dma_start(ea_in[:, b, :, :],
                                     a["edge_attr"].rearrange("(c e) w -> e c w", e=P)[
                                         :, bass.ds(it * GROUP + q * ROUND, ROUND), :]).then_inc(mean_loaded[b], 16)
                        flags = new_segment if n == 0 else same_segment
                        sp.dma_start(ea_flag[:, b, :],
                                     flags[bass.ds(at, ROUND * P)].unsqueeze(0).to_broadcast([EA, ROUND * P])
                                     ).then_inc(mean_loaded[b], 16)

            sp.wait_ge(pre.flags_stored, 32)
            mean_loads(0)
            with sp.Fori(0, NTG) as i:
                sp.wait_ge(n1.rows, i + 1)
                sp.dma_start(table.rearrange("(t p) w -> p t w", p=P)[:, bass.ds(i * TG, TG), :],
                             H[:, bass.ds(i * TG, TG), :]).then_inc(n1.stored, 16)
            mean_loads(1)
            with sp.Fori(0, NTG) as i:
                sp.wait_ge(n2.rows, i + 1)
                sp.dma_start(table.rearrange("(t p) w -> p t w", p=P)[:, bass.ds(i * TG, TG), :],
                             H[:, bass.ds(i * TG, TG), :]).then_inc(n2.stored, 16)
            sp.wait_ge(pre.changes_stored, 16)
            sp.wait_ge(pre.masks_stored, 16)
            sp.wait_ge(pre.dst_stored, 32)

            def load_dst(slot):
                sp.dma_start(pick_t, dst_rows[bass.ds(slot, GROUP), :].unsqueeze(0).to_broadcast([P, GROUP, P])
                             ).then_inc(att.rows_loaded, 16)

            sp.sem_inc(att.used, FREE)
            for n in range(LAYERS):
                load_dst(0)
                with sp.Fori(0, PAIRS) as it:
                    for b in range(2):
                        sp.wait_ge(att.used, n * NG + it * 2 + b + FREE)
                        slot = it * (2 * GROUP) + b * GROUP
                        for view, col in ((start_flag, 0), (end_flag, 1)):
                            sp.dma_start(view[:, b, :].rearrange("s (h e) -> s h e", h=HEADS),
                                         change_rows[bass.ds(slot, GROUP), col:col + P].unsqueeze(1)
                                         .to_broadcast([GROUP, HEADS, P])).then_inc(att_flags[b], 16)
                        sp.dma_start(masks[:, b, :, :],
                                     slot_masks[:, bass.ds(slot, GROUP + 1)].unsqueeze(0)
                                     .to_broadcast([HEADS, 3, GROUP + 1])).then_inc(att_flags[b], 16)
                        sp.wait_ge(att.dst_scored, n * (NG + 1) + it * 2 + b + 1)
                        load_dst(slot + GROUP)
                if n < LAYERS - 1:
                    with sp.Fori(0, NTG) as i:
                        sp.wait_ge(n3.rows, n * NTG + i + 1)
                        sp.dma_start(table.rearrange("(t p) w -> p t w", p=P)[:, bass.ds(i * TG, TG), :],
                                     H[:, bass.ds(i * TG, TG), :]).then_inc(n3.stored, 16)
            with sp.Fori(0, NTG) as i:
                sp.wait_ge(n3.rows, (LAYERS - 1) * NTG + i + 1)
                sp.dma_start(out.rearrange("(t p) w -> p t w", p=P)[:, bass.ds(i * TG, TG), :],
                             X[:, bass.ds(i * TG, TG), :]).then_inc(n3.stored, 16)
            sp.wait_ge(n3.stored, 16 * LAYERS * NTG)

        @block.gpsimd
        def _(pool):
            pool.memset(att_vec[:, :, :], 0.0).then_inc(pre.zeroed, 1)
            pool.iota(iota_i[:, :], pattern=[[1, P]], base=0, channel_multiplier=0).then_inc(pre.iota, 1)
            pool.iota(iota_s[:, 0:1], pattern=[[0, 1]], base=0, channel_multiplier=1).then_inc(pre.iota, 1)
            pool.iota(iota_s[:, 1:1 + NB], pattern=[[P, NB]], base=0, channel_multiplier=1).then_inc(pre.iota, 1)
            pool.iota(iota_nodes[:, :], pattern=[[P, NT]], base=0, channel_multiplier=1).then_inc(pre.iota, 1)
            pool.wait_ge(pre.firsts_stored, 16)
            pool.wait_ge(pre.indexed, 1)
            for k in range(NB):
                pool.indirect_dma_start(sd_row[:, k, :], None, a["chunks"],
                                        bass.IndirectOffsetOnAxis(chunk_idx[:, k:k + 1], 0)
                                        ).then_inc(pre.rows_gathered, 16)
            for k in range(NB):
                pool.indirect_dma_start(first_of[:, k:k + 1], None, slot_first,
                                        bass.IndirectOffsetOnAxis(chunk_idx[:, k:k + 1], 0)
                                        ).then_inc(pre.firsts_gathered, 16)

            def mean_gathers(n):
                with pool.Fori(0, NG) as it:
                    for q in range(RNG):
                        pool.wait_ge(mean.staged, n * (ROUNDS + RNG - 1) + it * RNG + q + 1)
                        pool.sem_inc(tick, 1)
                        for k in range(q * ROUND, (q + 1) * ROUND):
                            pool.indirect_dma_start(gathered[:, k, :], None, table,
                                                    bass.IndirectOffsetOnAxis(staged_idx[:, k:k + 1], 0)
                                                    ).then_inc(mean_gathered[q], 16)

            pool.wait_ge(n0.stored, 16 * NTG)
            pool.wait_ge(pre.masks_stored, 16)
            mean_gathers(0)
            pool.wait_ge(n1.stored, 16 * NTG)
            mean_gathers(1)
            for n in range(LAYERS):
                if n == 0:
                    pool.wait_ge(n2.stored, 16 * NTG)
                else:
                    pool.wait_ge(n3.stored, 16 * NTG * n)
                if n == 0:
                    pool.sem_inc(att.summed, 2 * GROUP)
                with pool.Fori(0, PAIRS) as it:
                    for b in range(2):
                        pool.wait_ge(att.staged, n * (NG + 2) + it * 2 + b + 1)
                        for q in range(RNG):
                            pool.wait_ge(att.summed, n * NS + it * (2 * GROUP) + b * GROUP + (q + 1) * ROUND)
                            pool.sem_inc(tick, 1)
                            for k in range(q * ROUND, (q + 1) * ROUND):
                                at = b * GROUP + k
                                pool.indirect_dma_start(gathered[:, at, :], None, table,
                                                        bass.IndirectOffsetOnAxis(staged_idx[:, at:at + 1], 0)
                                                        ).then_inc(att_gathered[n][b], 16)
            pool.wait_ge(att.summed, 2 * GROUP + LAYERS * NS)
            pool.wait_ge(mean_stored[0], 16 * (ROUNDS + FREE))
            pool.wait_ge(mean_stored[1], 16 * (ROUNDS + FREE))
            pool.sem_inc(tick, 1)
            for t in range(NT):
                pool.indirect_dma_start(node_stats_in[:, t, :], None, edge_stats,
                                        bass.IndirectOffsetOnAxis(last_row[:, t:t + 1], 0)
                                        ).then_inc(n3.stats_gathered, 16)

        @block.scalar
        def _(act):
            def turned_copy(src, dst, wait, count, done):
                act.wait_ge(wait, count)
                nc.scalar.copy(dst, src).then_inc(done, 1)

            def square_root(s, base):
                with act.Fori(0, NTG) as i:
                    act.wait_ge(s.var, base + i + 1)
                    nc.scalar.activation(small[:, 2, :], small[:, 1, :], ACT.Sqrt).then_inc(s.root, 1)

            act.wait_ge(pre.turned_a, 2 * NB)
            nc.scalar.copy(dst_local[:, 0:NR], rows_a[:, 0:NR]).then_inc(pre.copied_a, 1)
            nc.scalar.copy(src_of[:, 0:NR], rows_b[:, 0:NR]).then_inc(pre.copied_a, 1)
            square_root(n0, 0)

            def stage(n, r, q):
                nc.scalar.copy(staged_idx[:, q * ROUND:(q + 1) * ROUND],
                               src_of[:, bass.ds(r * ROUND, ROUND)] if not isinstance(r, int) else
                               src_of[:, r * ROUND:(r + 1) * ROUND]).then_inc(mean.staged, 1)

            def mean_scalar(n):
                if n == 0:
                    act.wait_ge(pre.tail_zeroed, 1)
                    act.sem_inc(mean.summed, FREE)
                    for stored in mean_stored:
                        act.sem_inc(stored, 16 * FREE)
                for r in range(RNG - 1):
                    stage(n, r, r)
                with act.Fori(0, NG) as it:
                    for q in range(RNG):
                        b = q % 2
                        act.wait_ge(mean.summed, n * NS + it * GROUP + q * ROUND + FREE)
                        stage(n, it * RNG + q + RNG - 1, (q + RNG - 1) % RNG)
                        act.wait_ge(mean.turned_back, n * ROUNDS + it * RNG + q + 1 + FREE)
                        act.wait_ge(mean_stored[b], 16 * (n * (ROUNDS // 2) + q // 2 + FREE) + it * (16 * RNG // 2))
                        nc.scalar.copy(ea_out[:, b, :], bank[:, 2 + b, 0:ROUND * EA]).then_inc(mean.copied, 1)
                        act.wait_ge(mean.copied, n * ROUNDS + it * RNG + q + 1 + FREE)
                        col = EA if n == 0 else 0
                        act.dma_start(edge_stats.rearrange("(c e) w -> e c w", e=P)[
                            :, bass.ds(it * GROUP + q * ROUND, ROUND), col:col + EA],
                            ea_out[:, b, :].rearrange("p (c w) -> p c w", w=EA)).then_inc(mean_stored[b], 16)

            def stores_landed(eng, n):
                for b in range(2):
                    eng.wait_ge(mean_stored[b], 16 * ((n + 1) * (ROUNDS // 2) + FREE))

            mean_scalar(0)
            stores_landed(act, 0)
            with act.Fori(0, NTG) as i:
                act.wait_ge(n1.turned, i + 1)
                nc.scalar.copy(tr_a[:, :, :], bank[:, 0:TG, 0:P]).then_inc(n1.copied, 1)
                nc.scalar.copy(tr_b[:, :, :], bank[:, 0:TG, P:2 * P]).then_inc(n1.copied, 1)
                act.wait_ge(n1.var, i + 1)
                nc.scalar.activation(small[:, 2, :], small[:, 1, :], ACT.Sqrt).then_inc(n1.root, 1)
            mean_scalar(1)
            stores_landed(act, 1)
            with act.Fori(0, NTG) as i:
                act.wait_ge(n2.turned, i + 1)
                nc.scalar.copy(tr_a[:, :, :], bank[:, 0:TG, 0:P]).then_inc(n2.copied, 1)
                nc.scalar.copy(tr_b[:, :, :], bank[:, 0:TG, P:2 * P]).then_inc(n2.copied, 1)
                act.wait_ge(n2.product, i + 1)
                nc.scalar.activation(acc_t[:, bass.ds(i * TG, TG), 0:D], bank[:, 0:TG, 2 * P:3 * P],
                                     ACT.Gelu).then_inc(n2.gelu, 1)
            act.wait_ge(n2.colvar, 1)
            nc.scalar.activation(sq[:, 1, :], sq[:, 0, :], ACT.Sqrt).then_inc(n2.colvar, 1)

            def att_copies(s, k):
                with act.Fori(0, NTG) as i:
                    act.wait_ge(s.var, k + i + 1)

            with act.Fori(0, NTG) as i:
                act.wait_ge(n2.var, i + 1)
                nc.scalar.activation(small[:, 2, :], small[:, 1, :], ACT.Sqrt).then_inc(n2.root, 1)
                act.wait_ge(n2.turned2, i + 1)
                nc.scalar.copy(tr_a[:, :, :], bank[:, 0:TG, 0:P]).then_inc(n2.copied2, 1)

            def act_picks(where, slot):
                for k in range(ROUND):
                    nc.scalar.activation(pick_dist[:, k, :], col_index[:, :], ACT.Abs, scale=-1.0,
                                         bias=dst_local[:, bass.ds(slot + k, 1)])
                act.drain()
                nc.scalar.activation(pick[:, where:where + ROUND, :], pick_dist[:, :, :], ACT.Relu, scale=-1.0,
                                     bias=ones[:, 0:1]).then_inc(att.picked, 1)
                act.drain()

            for n in range(LAYERS):
                for b in range(2):
                    nc.scalar.copy(staged_idx[:, b * GROUP:(b + 1) * GROUP],
                                   src_of[:, b * GROUP:(b + 1) * GROUP]).then_inc(att.staged, 1)

                for q in range(RNG):
                    act_picks(q * ROUND, q * ROUND)
                with act.Fori(0, PAIRS) as it:
                    for b in range(2):
                        act.wait_ge(att_gathered[n][b], 16 * GROUP + it * (16 * GROUP))
                        nc.scalar.copy(staged_idx[:, b * GROUP:(b + 1) * GROUP],
                                       src_of[:, bass.ds(it * (2 * GROUP) + (b + 2) * GROUP, GROUP)]
                                       ).then_inc(att.staged, 1)
                        act.wait_ge(att.shifted, n * NG + it * 2 + b + 1)
                        nc.scalar.activation(prob[:, :, :], score[:, :, :], ACT.Exp).then_inc(att.prob, 1)
                        act.wait_ge(att.scale_rows, n * NG + it * 2 + b + 1)
                        nc.scalar.activation(old_scale[:, :], bank[:, 5, 128:128 + HEADS], ACT.Exp
                                             ).then_inc(att.scale, 1)
                        slot = it * (2 * GROUP) + (b + 1) * GROUP
                        for q in range(RNG):
                            act.wait_ge(att.summed, 2 * GROUP + n * NS + slot - GROUP + (q + 1) * ROUND)
                            act_picks(q * ROUND, slot + q * ROUND)
                with act.Fori(0, NTG) as i:
                    act.wait_ge(n3.scored, n * 2 * NTG + i * 2 + 1)
                    nc.scalar.activation(selfs[:, 3:5, :, :], selfs[:, 3:5, :, :], ACT.Exp).then_inc(n3.weights, 1)
                    act.wait_ge(n3.scored, n * 2 * NTG + i * 2 + 2)
                    nc.scalar.activation(sq[:, :, :], sq[:, :, :], ACT.Exp).then_inc(n3.weights, 1)
                    if n < LAYERS - 1:
                        act.wait_ge(n3.turned, n * NTG + i + 1)
                        nc.scalar.copy(tr_a[:, :, :], bank[:, 0:TG, 0:P]).then_inc(n3.copied, 1)
                    else:
                        act.wait_ge(n3.var, i + 1)
                        nc.scalar.activation(small[:, 2, :], small[:, 1, :], ACT.Sqrt).then_inc(n3.root, 1)
                        act.wait_ge(n3.turned, n * NTG + i + 1)
                        nc.scalar.copy(tr_a[:, :, :], bank[:, 0:TG, 0:P])
                        nc.scalar.copy(tr_b[0:2 * EA, :, :], bank[0:2 * EA, 0:TG, P:2 * P])
                        nc.scalar.copy(tr_c[:, :, :], bank[0:EA, 0:TG, 2 * P:3 * P]).then_inc(n3.copied, 1)
                        for m in range(2):
                            act.wait_ge(n3.hidden, i * 2 + m + 1)
                            nc.scalar.activation(hid[:, m, :].rearrange("p (c n) -> p c n", c=2),
                                                 bank[:, 2 * m:2 * m + 2, 0:TG * P // 2], ACT.Relu,
                                                 bias=b1[:, m:m + 1]).then_inc(n3.relu, 1)

        @block.tensor
        def _(pe):
            pe.wait_ge(pre.counted, 1)
            pe.matmul(bank[:, 0, 0:NB], tri_strict[:, :], count, start=True, stop=True)
            pe.matmul(bank[:, 1, 0:NB], ones[:, :], count, start=True, stop=True).then_inc(pre.prefixed, 1)
            pe.wait_ge(pre.placed, 2)
            for k in range(NB):
                pe.matmul(rows_b[:, k * P:(k + 1) * P], ones[:, :], diag[:, k, :],
                          start=True, stop=True).then_inc(pre.spread, 1)
            pe.wait_ge(pre.split, 1)
            for k in range(NB):
                pe.transpose(rows_a[:, k * P:(k + 1) * P], dst_row[:, k, 0:P], ident[:, :]).then_inc(pre.turned_a, 1)
                pe.transpose(rows_b[:, k * P:(k + 1) * P], src_row[:, k, :], ident[:, :]).then_inc(pre.turned_a, 1)
            pe.wait_ge(pre.copied_a, 2)
            for k in range(NB):
                pe.transpose(rows_a[:, k * P:(k + 1) * P], is_last[:, k, :], ident[:, :]).then_inc(pre.turned_b, 1)
            for k in range(NB):
                pe.matmul(rows_b[0:33, k * P:(k + 1) * P], tile_cols[:, k, :], ident[:, :],
                          start=True, stop=True).then_inc(pre.turned_b, 1)
            pe.wait_ge(pre.copied_b, 2)
            for k in range(NB):
                pe.matmul(rows_a[0:1, k * P:(k + 1) * P], end_cols[:, 0, k:k + 1], ident[:, :],
                          start=True, stop=True).then_inc(pre.ends_turned, 1)
            for k in range(NB):
                pe.matmul(rows_b[0:1, k * P:(k + 1) * P], end_cols[:, 1, k:k + 1], ident[:, :],
                          start=True, stop=True).then_inc(pre.ends_turned, 1)
            pe.wait_ge(pre.masks_ready, 1)
            pe.wait_ge(pre.weights_loaded, 16 * WEIGHTS)
            for n in range(LAYERS):
                pe.transpose(bank[:, n, 0:P], w_att[:, n, 0:D], ident[:, :]).then_inc(pre.w_turned, 1)
            pe.wait_ge(pre.w_copied, 1)
            for n in range(LAYERS):
                pe.matmul(bank[:, 4 + n, 0:2 * HEADS], tr_a[:, n, :], att_vec[:, n, :],
                          start=True, stop=True).then_inc(pre.w_made, 1)
            for m in range(2):
                pe.matmul(bank[:, 7, m:m + 1], w1[0:UD, 3, m * P:(m + 1) * P], u0[:, :],
                          start=True, stop=True).then_inc(pre.w_made, 1)
            pe.wait_ge(pre.w_kept, 1)

            def mean_tensor(n):
                if n == 0:
                    pe.sem_inc(mean.added, FREE_BANKS)
                    pe.sem_inc(mean.scanned, FREE)
                    pe.sem_inc(mean.copied, FREE)
                with pe.Fori(0, NG) as it:
                    for q in range(RNG):
                        b = q % 2
                        r = n * ROUNDS + q
                        pe.wait_ge(mean_loaded[b], 32 * (n * (ROUNDS // 2) + q // 2 + 1) + it * (32 * RNG // 2))
                        pe.wait_ge(mean.scanned, it * RNG + r + FREE)
                        pe.sem_inc(pe_tick, 1)
                        for c in range(ROUND):
                            mm = pe.transpose(bank[0:EA, c // 4, (c % 4) * P:(c % 4 + 1) * P], ea_in[:, b, c, :],
                                              ident[:, :])
                        mm.then_inc(mean.turned, 1)
                        pe.wait_ge(mean_gathered[q], 16 * ROUND * (n * NG + 1) + it * (16 * ROUND))
                        pe.wait_ge(mean.picked, it * RNG + r + 1)
                        for c in range(ROUND):
                            k = q * ROUND + c
                            pe.wait_ge(mean.added, n * NS + it * GROUP + k + 1)
                            pe.matmul(bank[:, 4 + k % 4, 0:MEAN_W], pick[:, k, :], gathered[:, k, 0:MEAN_W],
                                      start=True, stop=True).then_inc(mean.summed, 1)
                        pe.wait_ge(mean.scanned, it * RNG + r + 1 + FREE)
                        pe.wait_ge(mean.copied, it * RNG + r + FREE)
                        pe.sem_inc(pe_tick, 1)
                        for c in range(ROUND):
                            mm = pe.transpose(bank[:, 2 + b, c * EA:(c + 1) * EA], ea_scan[:, c * P:(c + 1) * P],
                                              ident[0:EA, 0:EA])
                        mm.then_inc(mean.turned_back, 1)

            mean_tensor(0)
            pe.wait_ge(n1.degrees, 1)
            pe.matmul(bank[:, 7, 0:NT], tri[:, :], degree, start=True, stop=True)
            pe.matmul(bank[:, 7, 64:64 + NT], ones[:, :], degree, start=True, stop=True).then_inc(n1.prefixed, 1)

            def banks_left(n):
                pe.wait_ge(mean.copied, (n + 1) * ROUNDS + FREE)
                pe.wait_ge(mean.added, FREE_BANKS + (n + 1) * NS)

            banks_left(0)

            def two_products(s, i, wa, wb, bias):
                pe.wait_ge(s.scaled, i + 1)
                for t in range(TG):
                    pe.transpose(bank[:, t, 0:P], sq[:, t, :], ident[:, :])
                for t in range(TG):
                    mm = pe.transpose(bank[:, t, P:2 * P], xn[:, t, :], ident[:, :])
                mm.then_inc(s.turned, 1)
                pe.wait_ge(s.copied, 2 * i + 2)
                for t in range(TG):
                    pe.matmul(bank[:, t, 2 * P:3 * P], tr_a[:, t, :], wa, start=True, stop=False)
                    pe.matmul(bank[:, t, 2 * P:3 * P], tr_b[:, t, :], wb, start=False, stop=False)
                    mm = pe.matmul(bank[:, t, 2 * P:3 * P], ones[0:1, :], bias, start=False, stop=True)
                mm.then_inc(s.product, 1)

            with pe.Fori(0, NTG) as i:
                two_products(n1, i, w_neigh[:, :], w_self[:, :], bias_row[0:1, 0, :])
            mean_tensor(1)
            banks_left(1)
            with pe.Fori(0, NTG) as i:
                two_products(n2, i, w_l[:, :], w_r[:, :], bias_row[0:1, 1, :])
            pe.wait_ge(n2.centred, 1)
            pe.matmul(bank[:, 7, 0:D], ones[:, :], sq[:, 0, :], start=True, stop=True).then_inc(n2.colsum, 1)
            pe.wait_ge(n2.squares, 1)
            pe.matmul(bank[:, 7, D:2 * D], ones[:, :], sq[:, 0, :], start=True, stop=True).then_inc(n2.colsum, 1)

            def table_rows(ready, turned, copied, product, i, base, n):
                pe.wait_ge(ready, base + i + 1)
                for t in range(TG):
                    mm = pe.transpose(bank[:, t, 0:P], xn[:, t, :], ident[:, :])
                mm.then_inc(turned, 1)
                pe.wait_ge(copied, base + i + 1)
                for t in range(TG):
                    mm = pe.matmul(bank[:, t, P:2 * P + 2 * HEADS], tr_a[:, t, :], w_att[:, n, :],
                                   start=True, stop=True)
                mm.then_inc(product, 1)

            with pe.Fori(0, NTG) as i:
                table_rows(n2.next, n2.turned2, n2.copied2, n2.product2, i, 0, 0)

            for n in range(LAYERS):
                def score_quarter(j, slot):
                    _, at = nc.values_load_multi_w_load_instructions(
                        offsets[32:33, bass.ds(slot + 4 * j, 4)], engines=[PE_E], min_val=0,
                        max_val=(NT - 1) * PARTS * HEADS, skip_runtime_bounds_check_because=BOUNDED)
                    for k in range(4 * j, 4 * j + 4):
                        for part_no in range(PARTS):
                            mm = pe.matmul(bank[:, 2, k * HEADS:(k + 1) * HEADS], pick_t[:, k, :],
                                           dst_parts[:, bass.ds(at[k % 4] + part_no * HEADS, HEADS)],
                                           start=part_no == 0, stop=part_no == PARTS - 1)
                    if j == QG - 1:
                        mm.then_inc(att.dst_scored, 1)

                if n == 0:
                    pe.sem_inc(att.added, FREE_BANKS)
                pe.wait_ge(att.turned, n * 2 * (NG + 1) + 2)
                for j in range(QG):
                    score_quarter(j, 0)
                with pe.Fori(0, PAIRS) as it:
                    for b in range(2):
                        done = n * NG + it * 2 + b
                        pe.wait_ge(att.scored, done + 1)
                        for h in range(HEADS):
                            mm = pe.transpose(bank[0:GROUP, 3, h * P:(h + 1) * P], score[:, h, :], ident[:, :])
                        mm.then_inc(att.score_rows, 1)
                        pe.wait_ge(att.firsts, done + 1)
                        pe.sem_inc(pe_tick, 1)
                        pe.transpose(bank[0:HEADS, 5, 0:GROUP], seg_f[:, P - 1::P],
                                     ident[0:GROUP, 0:GROUP])
                        pe.transpose(bank[0:HEADS, 5, GROUP:2 * GROUP], seg_m[:, 0::P],
                                     ident[0:GROUP, 0:GROUP]).then_inc(att.ends, 1)
                        pe.wait_ge(att.crossed, done + 1)
                        pe.sem_inc(pe_tick, 1)
                        pe.transpose(bank[0:GROUP, 5, 64:64 + HEADS], cross[:, 0, :], ident[0:HEADS, 0:HEADS])
                        pe.transpose(bank[0:GROUP, 5, 68:68 + HEADS], cross[:, 1, :],
                                     ident[0:HEADS, 0:HEADS]).then_inc(att.cross_rows, 1)
                        pe.wait_ge(att.maxima, done + 1)
                        pe.sem_inc(pe_tick, 1)
                        for h in range(HEADS):
                            mm = pe.transpose(bank[:, 4, h * GROUP:(h + 1) * GROUP],
                                              seg_m[:, h * P:(h + 1) * P], ident[0:GROUP, 0:GROUP])
                        mm.then_inc(att.max_back, 1)
                        picks = n * (NG + 1) * RNG + it * (2 * RNG) + b * RNG
                        pe.wait_ge(att.picked, picks + 1)
                        pe.wait_ge(att.log_scale, done + 1)
                        pe.matmul(bank[:, 5, 128:128 + HEADS], pick[0:1, 0, :], log_scale[:, :],
                                  start=True, stop=True).then_inc(att.scale_rows, 1)
                        for k in range(GROUP):
                            first = n * NS + it * (2 * GROUP) + b * GROUP
                            if k % ROUND == 0:
                                pe.wait_ge(att.picked, picks + k // ROUND + 1)
                            pe.wait_ge(att.weighted, first + k + 1)
                            pe.wait_ge(att.added, first + k + 1)
                            pe.matmul(bank[:, 4 + k % 4, 0:ROW], pick[:, k, :], gathered[:, b * GROUP + k, :],
                                      start=True, stop=True).then_inc(att.summed, 1)
                            if k == 3:
                                pe.wait_ge(att.turned, n * 2 * (NG + 1) + it * 4 + 2 * (b + 2))
                            if k % 4 == 3:
                                score_quarter(k // 4, it * (2 * GROUP) + (b + 1) * GROUP)
                if n < LAYERS - 1:
                    with pe.Fori(0, NTG) as i:
                        table_rows(n3.next, n3.turned, n3.copied, n3.product, i, n * NTG, n + 1)
            with pe.Fori(0, NTG) as i:
                base = (LAYERS - 1) * NTG
                pe.wait_ge(n3.next, base + i + 1)
                for t in range(TG):
                    pe.transpose(bank[:, t, 0:P], xn[:, t, :], ident[:, :])
                    pe.transpose(bank[0:2 * EA, t, P:2 * P], cat[:, t, 0:2 * EA], ident[:, :])
                    mm = pe.transpose(bank[0:EA, t, 2 * P:3 * P], cat[:, t, 2 * EA:3 * EA], ident[:, :])
                mm.then_inc(n3.turned, 1)
                pe.wait_ge(n3.copied, base + i + 1)
                half = TG * P // 2
                for m in range(2):
                    for c in range(2):
                        for part_no, (rows, tr) in enumerate(((P, tr_a), (2 * EA, tr_b), (EA, tr_c))):
                            mm = pe.matmul(bank[:, 2 * m + c, 0:half],
                                           w1[0:rows, part_no, m * P:(m + 1) * P],
                                           tr[0:rows, :, :].rearrange("p t n -> p (t n)")[:, c * half:(c + 1) * half],
                                           start=(part_no == 0), stop=(part_no == 2))
                    mm.then_inc(n3.hidden, 1)
                pe.wait_ge(n3.relu, 2 * i + 2)
                for t in range(TG):
                    for m in range(2):
                        pe.matmul(bank[:, t, 0:P], hid[:, m, t * P:(t + 1) * P], w2[:, m, :],
                                  start=(m == 0), stop=False)
                    mm = pe.matmul(bank[:, t, 0:P], ones[0:1, :], bias_row[0:1, 2, :], start=False, stop=True)
                mm.then_inc(n3.product, 1)

        @block.vector
        def _(dve):
            def then(*_):
                dve.drain()

            dve.wait_ge(pre.iota, 4)
            dve.tensor_copy(col_index[:, :], iota_i[:, :])
            dve.tensor_copy(part_index[:, :], iota_s[:, 0:1])
            dve.tensor_copy(slot_no, iota_s[:, 1:1 + NB])
            dve.memset(ones[:, :], 1.0)
            then()
            dve.tensor_scalar(ident[:, :], col_index[:, :], part_index[:, 0:1], None, ALU.is_equal)
            dve.tensor_scalar(tri_strict[:, :], col_index[:, :], part_index[:, 0:1], None, ALU.is_gt)
            dve.tensor_scalar(tri[:, :], col_index[:, :], part_index[:, 0:1], None, ALU.is_ge)
            dve.wait_ge(pre.tables_loaded, 32)
            dve.tensor_scalar(int_tmp[:, :, :], edge_now[:, :, 0::P - 1], 7, None, ALU.arith_shift_right)
            then()
            dve.tensor_copy(chunk_tile, int_tmp[:, :, 0])
            dve.tensor_copy(chunk_last, int_tmp[:, :, 1])
            then()
            dve.tensor_tensor(count, chunk_last, chunk_tile, ALU.subtract)
            then()
            dve.tensor_scalar(count, count, 1.0, None, ALU.add).then_inc(pre.counted, 1)
            dve.tensor_tensor(edge_cmp, edge_now, edge_before, ALU.is_equal)
            then()
            dve.tensor_copy(flag_b, edge_cmp)
            then()
            dve.tensor_scalar(flag_a, flag_b, 1.0, -EDGE_FAR, ALU.subtract, ALU.mult).then_inc(pre.edge_flags, 1)
            dve.wait_ge(pre.prefixed, 1)
            dve.tensor_copy(before, bank[:, 0, 0:NB])
            dve.tensor_copy(total, bank[:, 1, 0:NB])
            then()
            dve.tensor_tensor_scan(upto, ones[:, 0:NB], total, 0.0, ALU.mult, ALU.add)
            then()
            dve.tensor_tensor(before, before, upto, ALU.add)
            then()
            dve.tensor_tensor(before, before, total, ALU.subtract).then_inc(pre.placed, 1)
            then()
            dve.tensor_tensor(diag, ident[:, :].unsqueeze(1).to_broadcast([P, NB, P]),
                              before.unsqueeze(2).to_broadcast([P, NB, P]), ALU.mult).then_inc(pre.placed, 1)
            dve.wait_ge(pre.spread, NB)
            dve.tensor_copy(first_row, rows_b[:, 0:NR])
            then()
            for k in range(NB):
                dve.tensor_scalar(scratch, first_row, slot_no[:, k:k + 1], 0.0, ALU.is_le, ALU.add,
                                  accum_out=slots_to[:, k:k + 1])
                then()
            dve.tensor_scalar(chunk_of, slots_to, 1.0, None, ALU.subtract)
            then()
            dve.tensor_copy(chunk_idx[:, :], chunk_of).then_inc(pre.indexed, 1)

            def layer_norm(x_view, out_view, s, count_at):
                dve.tensor_reduce(small[:, 0, :], x_view, AX.X, ALU.add)
                then()
                dve.tensor_scalar(small[:, 0, :], small[:, 0, :], 1.0 / D, None, ALU.mult)
                then()
                dve.tensor_tensor(xc[:, :, :], x_view, small[:, 0, :].unsqueeze(2).to_broadcast([P, TG, D]),
                                  ALU.subtract)
                then()
                dve.tensor_tensor(sq[:, :, :], xc[:, :, :], xc[:, :, :], ALU.mult)
                then()
                dve.tensor_reduce(small[:, 1, :], sq[:, :, :], AX.X, ALU.add)
                then()
                dve.tensor_scalar(small[:, 1, :], small[:, 1, :], 1.0 / D, EPS, ALU.mult, ALU.add).then_inc(s.var, 1)
                dve.wait_ge(s.root, count_at)
                dve.reciprocal(small[:, 3, :], small[:, 2, :])
                then()
                return dve.scalar_tensor_tensor(out=out_view, in0=xc[:, :, :], scalar=0.0,
                                                in1=small[:, 3, :].unsqueeze(2).to_broadcast([P, TG, D]),
                                                op0=ALU.max, op1=ALU.mult)

            dve.wait_ge(pre.rows_gathered, 16 * NB)
            dve.wait_ge(pre.firsts_gathered, 16 * NB)
            dve.tensor_copy(src_row, sd_row[:, :, 0:P])
            dve.tensor_copy(dst_row, sd_row[:, :, P:2 * P + 1])
            dve.tensor_scalar(int_tmp[:, :, 0], sd_row[:, :, P], 7, None, ALU.arith_shift_right)
            then()
            dve.tensor_copy(tile_of, int_tmp[:, :, 0])
            dve.tensor_tensor(tmp, slot_no, first_of, ALU.subtract)
            dve.tensor_copy(end_cols[:, 0, :], dst_row[:, :, 0])
            dve.tensor_copy(end_cols[:, 1, :], dst_row[:, :, P - 1])
            dve.tensor_tensor(is_last, dst_row[:, :, 0:P], dst_row[:, :, 1:P + 1], ALU.not_equal)
            then()
            dve.tensor_tensor(tile_of, tile_of, tmp, ALU.add)
            dve.memset(change[:, :, 0:1], FAR)
            dve.memset(change[:, :, P:P + 1], FAR)
            dve.tensor_scalar(change[:, :, 1:P], is_last[:, :, 0:P - 1], FAR, None, ALU.mult)
            then()
            dve.tensor_scalar(tmp, tile_of, float(P), None, ALU.mult)
            dve.wait_ge(pre.flags_stored, 32)
            dve.tensor_copy(change_keep, change).then_inc(pre.changes, 1)
            dve.tensor_scalar(tile_of, tile_of, float(NT - 1), None, ALU.min)
            then()
            dve.tensor_tensor(dst_row[:, :, 0:P], dst_row[:, :, 0:P], tmp.unsqueeze(2).to_broadcast([P, NB, P]),
                              ALU.subtract)
            dve.memset(tile_cols[:, :, :], 0.0)
            dve.memset(dst_tail, -1.0)
            then()
            dve.tensor_copy(tile_cols[:, :, 0], tile_of)
            dve.tensor_copy(tile_cols[:, :, 32], tile_of).then_inc(pre.split, 1)
            dve.tensor_copy(dst_bf, dst_row[:, :, 0:P]).then_inc(pre.dst_kept, 1)
            dve.memset(dst_local[:, NR:], -1.0)
            dve.memset(src_of[:, NR:], 0.0)
            dve.memset(last_edge[:, NR:], 0.0)
            dve.memset(offsets[:, :], 0).then_inc(pre.tail_zeroed, 1)
            then()
            dve.wait_ge(pre.turned_b, 2 * NB)
            dve.tensor_copy(last_edge[:, 0:NR], rows_a[:, 0:NR]).then_inc(pre.copied_b, 1)
            dve.tensor_scalar(offsets[0:1, 0:NR], rows_b[0:1, 0:NR], float(ROW), None, ALU.mult)
            dve.tensor_scalar(offsets[32:33, 0:NR], rows_b[32:33, 0:NR], float(PARTS * HEADS), None, ALU.mult
                              ).then_inc(pre.copied_b, 1)
            dve.wait_ge(pre.ends_turned, 2 * NB)
            dve.memset(masks_row, FAR)
            dve.memset(line_a, 0.0)
            dve.memset(line_b, 0.0)
            then()
            dve.tensor_copy(line_c, rows_a[0:1, 0:NR])
            dve.tensor_copy(line_d, rows_b[0:1, 0:NR])
            then()
            dve.tensor_tensor(line_a[:, 1:NR], line_c[:, 1:NR], line_d[:, 0:NR - 1], ALU.is_equal)
            dve.tensor_tensor(line_b[:, 0:NR], line_c, line_d, ALU.is_equal)
            then()
            dve.tensor_tensor(line_c, line_a[:, 0:NR], line_b[:, 0:NR], ALU.mult)
            dve.tensor_tensor(line_d[:, 0:NR - 1], line_a[:, 1:NR], line_b[:, 0:NR - 1], ALU.mult)
            then()
            dve.tensor_scalar(masks_row[:, 0, 0:NR], line_a[:, 0:NR], 1.0, -FAR, ALU.subtract, ALU.mult)
            dve.tensor_scalar(masks_row[:, 1, 0:NR], line_c, 1.0, -FAR, ALU.subtract, ALU.mult)
            dve.tensor_scalar(masks_row[:, 2, 0:NR - 1], line_d[:, 0:NR - 1], 1.0, -FAR, ALU.subtract, ALU.mult
                              ).then_inc(pre.masks_ready, 1)
            dve.wait_ge(pre.w_turned, LAYERS)
            dve.tensor_copy(tr_a[:, 0:LAYERS, :], bank[:, 0:LAYERS, 0:P]).then_inc(pre.w_copied, 1)
            dve.wait_ge(pre.w_made, LAYERS + 2)
            dve.tensor_copy(w_att[:, :, D:D + 2 * HEADS], bank[:, 4:4 + LAYERS, 0:2 * HEADS])
            dve.tensor_tensor(b1[:, :], b1[:, :], bank[:, 7, 0:2], ALU.add).then_inc(pre.w_kept, 1)
            dve.wait_ge(pre.x_loaded, 16)
            dve.wait_ge(pre.changes_stored, 16)
            dve.wait_ge(pre.dst_stored, 32)
            then()
            dve.memset(H[:, :, D:ROW], 1.0)
            with dve.Fori(0, NTG) as i:
                layer_norm(X[:, bass.ds(i * TG, TG), :], H[:, bass.ds(i * TG, TG), 0:D], n0, i + 1
                           ).then_inc(n0.rows, 1)
            then()
            dve.memset(acc[:, :], 0.0)
            dve.memset(ea_scan, 0.0)
            then()

            def build_picks(where, slot):
                return dve.tensor_tensor(pick[:, where:where + ROUND, :],
                                         dst_local[:, bass.ds(slot, ROUND)].unsqueeze(2).to_broadcast([P, ROUND, P]),
                                         col_index[:, :].unsqueeze(1).to_broadcast([P, ROUND, P]), ALU.is_equal)

            def add_sums(s, slot, base, k0, width):
                for k in range(k0, k0 + ROUND):
                    if k % 4 == 0:
                        _, at = nc.values_load_multi_w_load_instructions(
                            offsets[0:1, bass.ds(slot + k, 4)], engines=[DVE_E], min_val=0, max_val=(NT - 1) * ROW,
                            skip_runtime_bounds_check_because=BOUNDED)
                    row = acc[:, bass.ds(at[k % 4], width)]
                    dve.wait_ge(s.summed, base + k + 1)
                    dve.tensor_tensor(row, row, bank[:, 4 + k % 4, 0:width], ALU.add).then_inc(s.added, 1)
                    then()

            def add_sum(slot, summed, added, k):
                if k % 4 == 0:
                    _, at = nc.values_load_multi_w_load_instructions(
                        offsets[0:1, bass.ds(slot + k, 4)], engines=[DVE_E], min_val=0, max_val=(NT - 1) * ROW,
                        skip_runtime_bounds_check_because=BOUNDED)
                    tile_at[:] = at
                row = acc[:, bass.ds(tile_at[k % 4], ROW)]
                dve.wait_ge(att.added, added + k)
                dve.wait_ge(att.summed, summed + k + 1)
                dve.tensor_tensor(row, row, bank[:, 4 + k % 4, 0:ROW], ALU.add).then_inc(att.added, 1)

            tile_at = [None] * 4

            def mean_vector(n):
                if n == 0:
                    dve.sem_inc(mean.turned_back, FREE)
                with dve.Fori(0, NG) as it:
                    for q in range(RNG):
                        r = n * ROUNDS + q
                        build_picks(q * ROUND, it * GROUP + q * ROUND).then_inc(mean.picked, 1)
                        dve.wait_ge(mean.turned, it * RNG + r + 1)
                        dve.wait_ge(mean.turned_back, it * RNG + r + FREE)
                        for c in range(2):
                            scan = dve.tensor_tensor_scan(
                                ea_scan[:, c * 512:(c + 1) * 512], ea_flag[:, q % 2, c * 512:(c + 1) * 512],
                                bank[0:EA, c, :], ea_scan[:, 1023 - 512 * c:1024 - 512 * c],
                                ALU.add if n == 0 else ALU.mult, ALU.max if n == 0 else ALU.add)
                            if c == 0:
                                then()
                        scan.then_inc(mean.scanned, 1)
                        add_sums(mean, it * GROUP, n * NS + it * GROUP + FREE, q * ROUND, MEAN_W)

            def stores_landed(n):
                for b in range(2):
                    dve.wait_ge(mean_stored[b], 16 * ((n + 1) * (ROUNDS // 2) + FREE))
                dve.wait_ge(mean.turned_back, (n + 1) * ROUNDS + FREE)

            mean_vector(0)
            stores_landed(0)
            dve.tensor_copy(degree, acc_t[:, :, D]).then_inc(n1.degrees, 1)
            then()
            dve.tensor_scalar(inv_degree, degree, 1.0, None, ALU.max)
            dve.tensor_scalar(has_edge, degree, 1.0, None, ALU.min)
            then()
            dve.reciprocal(inv_degree, inv_degree)
            dve.tensor_scalar(no_edge_far, has_edge, 1.0, -FAR, ALU.subtract, ALU.mult)
            dve.wait_ge(n1.prefixed, 1)
            dve.tensor_copy(real_node, bank[:, 7, 64:64 + NT])
            then()
            dve.tensor_tensor_scan(rows_before, ones[:, 0:NT], real_node, -1.0, ALU.mult, ALU.add)
            then()
            dve.tensor_tensor(rows_before, rows_before, real_node, ALU.subtract)
            then()
            dve.tensor_tensor(rows_before, rows_before, bank[:, 7, 0:NT], ALU.add)
            then()
            dve.tensor_scalar(rows_before, rows_before, 0.0, None, ALU.max)
            dve.tensor_copy(real_node, iota_nodes[:, :])
            then()
            dve.tensor_copy(last_row[:, :], rows_before)
            dve.tensor_scalar(real_node, real_node, float(g.nodes), None, ALU.is_lt)
            then()

            def mean_of(i):
                dve.tensor_tensor(sq[:, :, :], acc_t[:, bass.ds(i * TG, TG), 0:D],
                                  inv_degree[:, bass.ds(i * TG, TG)].unsqueeze(2).to_broadcast([P, TG, D]), ALU.mult)
                return dve.tensor_copy(xn[:, :, :], H[:, bass.ds(i * TG, TG), 0:D])

            with dve.Fori(0, NTG) as i:
                mean_of(i).then_inc(n1.scaled, 1)
                dve.wait_ge(n1.product, i + 1)
                x_group = X[:, bass.ds(i * TG, TG), :]
                dve.tensor_tensor(x_group, x_group, bank[:, 0:TG, 2 * P:3 * P], ALU.add)
                then()
                layer_norm(x_group, H[:, bass.ds(i * TG, TG), 0:D], n1, i + 1).then_inc(n1.rows, 1)
                then()
            dve.memset(acc[:, :], 0.0)
            dve.memset(ea_scan, 0.0)
            then()
            mean_vector(1)
            stores_landed(1)

            with dve.Fori(0, NTG) as i:
                mean_of(i).then_inc(n2.scaled, 1)
                dve.wait_ge(n2.gelu, i + 1)
            for t in range(g.nodes // P, NT):
                dve.tensor_scalar(acc_t[:, t, 0:D], acc_t[:, t, 0:D], real_node[:, t:t + 1], None, ALU.mult)
            then()
            dve.tensor_reduce(sq[:, 0, :], acc_t[:, :, 0:D].rearrange("p t d -> p d t"), AX.X, ALU.add
                              ).then_inc(n2.centred, 1)
            dve.wait_ge(n2.colsum, 1)
            dve.scalar_tensor_tensor(out=sq[:, 2, :], in0=bank[:, 7, 0:D], scalar=1.0 / g.nodes,
                                     in1=norm_par[:, 2, :], op0=ALU.mult, op1=ALU.mult)
            then()
            dve.tensor_tensor(acc_t[:, :, 0:D], acc_t[:, :, 0:D],
                              sq[:, 2, :].unsqueeze(1).to_broadcast([P, NT, D]), ALU.subtract)
            then()
            for t in range(g.nodes // P, NT):
                dve.tensor_scalar(acc_t[:, t, 0:D], acc_t[:, t, 0:D], real_node[:, t:t + 1], None, ALU.mult)
            dve.memset(sq[:, 0, :], 0.0)
            then()
            with dve.Fori(0, NTG) as i:
                out_group = acc_t[:, bass.ds(i * TG, TG), 0:D]
                dve.tensor_tensor(xc[:, :, :], out_group, out_group, ALU.mult)
                then()
                dve.tensor_reduce(sq[:, 1, :], xc[:, :, :].rearrange("p t d -> p d t"), AX.X, ALU.add)
                then()
                dve.tensor_tensor(sq[:, 0, :], sq[:, 0, :], sq[:, 1, :], ALU.add)
                then()
            dve.memset(small[:, 3, 0:1], 0.0).then_inc(n2.squares, 1)
            dve.wait_ge(n2.colsum, 2)
            dve.tensor_scalar(sq[:, 0, :], bank[:, 7, D:2 * D], 1.0 / g.nodes, EPS, ALU.mult, ALU.add
                              ).then_inc(n2.colvar, 1)
            dve.wait_ge(n2.colvar, 2)
            dve.reciprocal(tr_b[:, 0, :], sq[:, 1, :])
            then()
            dve.tensor_tensor(tr_b[:, 0, :], tr_b[:, 0, :], norm_par[:, 0, :], ALU.mult)
            then()

            def write_rows(i, n):
                rows = H[:, bass.ds(i * TG, TG), :]
                head_rows = rows[:, :, 0:AW].rearrange("p t (h c) -> p t h c", h=HEADS)
                dve.sem_inc(dve_tick, 1)
                dve.tensor_copy(head_rows[:, :, :, 0:HC],
                                bank[:, 0:TG, P:2 * P].rearrange("p t (h c) -> p t h c", h=HEADS))
                dve.tensor_copy(head_rows[:, :, :, HC], ones[:, 0:TG * HEADS].rearrange("p (t h) -> p t h", t=TG))
                dst_scores = bank[:, 0:TG, 2 * P + HEADS:2 * P + 2 * HEADS]
                rest = selfs[:, 0, :, :]
                dve.tensor_copy(score_t[:, bass.ds(i * TG, TG), :], dst_scores)
                dve.tensor_copy(parts_t[:, bass.ds(i * TG, TG), 0, :], dst_scores)
                for part_no in range(1, PARTS):
                    then()
                    dve.tensor_tensor(rest, rest if part_no > 1 else dst_scores,
                                      parts_t[:, bass.ds(i * TG, TG), part_no - 1, :], ALU.subtract)
                    then()
                    dve.tensor_copy(parts_t[:, bass.ds(i * TG, TG), part_no, :], rest)
                return dve.tensor_copy(rows[:, :, AW:ROW], bank[:, 0:TG, 2 * P:2 * P + HEADS])

            with dve.Fori(0, NTG) as i:
                x_group = X[:, bass.ds(i * TG, TG), :]
                dve.tensor_tensor(xc[:, :, :], acc_t[:, bass.ds(i * TG, TG), 0:D],
                                  tr_b[:, 0, :].unsqueeze(1).to_broadcast([P, TG, D]), ALU.mult)
                dve.tensor_tensor(x_group, x_group, H[:, bass.ds(i * TG, TG), 0:D], ALU.add)
                then()
                dve.tensor_tensor(xc[:, :, :], xc[:, :, :],
                                  norm_par[:, 1, :].unsqueeze(1).to_broadcast([P, TG, D]), ALU.add)
                then()
                dve.tensor_tensor(x_group, x_group, xc[:, :, :], ALU.add)
                then()
                layer_norm(x_group, xn[:, :, :], n2, i + 1).then_inc(n2.next, 1)
                dve.wait_ge(n2.product2, i + 1)
                write_rows(i, 0).then_inc(n2.rows, 1)
                then()
            dve.memset(acc[:, :], 0.0)
            dve.memset(cross[:, :, :], 0.0)
            dve.memset(log_scale[:, :], 0.0)
            then()

            edp = bank[:, 2, 0:P].rearrange("p (s h) -> p h s", h=HEADS)
            back = bank[:, 4, 0:P].rearrange("p (h s) -> p h s", h=HEADS)
            grp = bank[0:GROUP, 3, :]

            for n in range(LAYERS):
                if n:
                    dve.memset(acc[:, :], 0.0)
                dve.memset(carry_f[:, :], FAR)
                dve.memset(carry_b[:, :], FAR)

                def build_pick_t(part_no):
                    ks = slice(part_no * GROUP // 2, (part_no + 1) * GROUP // 2)
                    dve.tensor_scalar(pick_t[:, ks, :], pick_t[:, ks, :], part_index[:, 0:1], None,
                                      ALU.is_equal).then_inc(att.turned, 1)

                dve.wait_ge(att.rows_loaded, 16 * (n * (NG + 1) + 1))
                for part_no in range(2):
                    build_pick_t(part_no)
                with dve.Fori(0, PAIRS) as it:
                    for b in range(2):
                        done = n * NG + it * 2 + b
                        slot = it * (2 * GROUP) + b * GROUP
                        rows = gathered[:, b * GROUP:(b + 1) * GROUP, :]
                        dve.wait_ge(att_gathered[n][b], 16 * GROUP + it * (16 * GROUP))
                        dve.wait_ge(att.dst_scored, n * (NG + 1) + it * 2 + b + 1)
                        dve.tensor_tensor(raw[:, :, :], rows[:, :, AW:ROW].rearrange("p s h -> p h s"), edp, ALU.add)
                        then()
                        dve.scalar_tensor_tensor(out=score[:, :, :], in0=raw[:, :, :], scalar=SLOPE,
                                                 in1=raw[:, :, :], op0=ALU.mult, op1=ALU.max
                                                 ).then_inc(att.scored, 1)
                        dve.wait_ge(att_flags[b], 48 * (n * PAIRS + 1) + it * 48)
                        dve.wait_ge(att.score_rows, done + 1)
                        dve.tensor_tensor_scan(seg_f, start_flag[:, b, :], grp, FAR, ALU.add, ALU.max)
                        then()
                        dve.tensor_tensor_scan(seg_m[:, ::-1], end_flag[:, b, ::-1], seg_f[:, ::-1], FAR,
                                               ALU.add, ALU.max).then_inc(att.firsts, 1)
                        dve.wait_ge(att.ends, done + 1)
                        dve.tensor_tensor_scan(carry_f[:, 1:GROUP + 1], masks[:, b, 1, 0:GROUP],
                                               bank[0:HEADS, 5, 0:GROUP], carry_f[:, 0:1], ALU.add, ALU.max)
                        dve.tensor_tensor_scan(carry_b[:, 0:GROUP][:, ::-1], masks[:, b, 2, 0:GROUP][:, ::-1],
                                               bank[0:HEADS, 5, GROUP:2 * GROUP][:, ::-1], FAR, ALU.add, ALU.max)
                        then()
                        dve.tensor_tensor(cross[:, 0, :], carry_f[:, 0:GROUP], masks[:, b, 0, 0:GROUP], ALU.add)
                        dve.tensor_tensor(cross[:, 1, :], carry_b[:, 1:GROUP + 1], masks[:, b, 0, 1:GROUP + 1],
                                          ALU.add).then_inc(att.crossed, 1)
                        dve.wait_ge(att.rows_loaded, 16 * (n * (NG + 1) + b + 2) + it * 32)
                        dve.wait_ge(att.dst_scored, n * (NG + 1) + it * 2 + b + 1)
                        build_pick_t(0)
                        then()
                        dve.tensor_copy(carry_f[:, 0:1], carry_f[:, GROUP:GROUP + 1])
                        dve.wait_ge(att.cross_rows, done + 1)
                        dve.tensor_copy(cross_rows[:, :], bank[0:GROUP, 5, 64:72])
                        dve.tensor_copy(grp_sb, grp)
                        then()
                        dve.tensor_tensor(grp_sb[:, 0::P], grp_sb[:, 0::P], cross_rows[:, 0:HEADS], ALU.max)
                        then()
                        dve.tensor_tensor(grp_sb[:, P - 1::P], grp_sb[:, P - 1::P], cross_rows[:, HEADS:2 * HEADS],
                                          ALU.max)
                        then()
                        dve.tensor_tensor_scan(seg_f, start_flag[:, b, :], grp_sb, FAR, ALU.add, ALU.max)
                        then()
                        dve.tensor_tensor_scan(seg_m[:, ::-1], end_flag[:, b, ::-1], seg_f[:, ::-1], FAR,
                                               ALU.add, ALU.max).then_inc(att.maxima, 1)
                        build_pick_t(1)
                        dve.wait_ge(att.max_back, done + 1)
                        dve.tensor_tensor(score[:, :, :], score[:, :, :], back, ALU.subtract
                                          ).then_inc(att.shifted, 1)
                        dve.tensor_tensor(log_scale[:, :], cross_rows[0:1, 0:HEADS], bank[0:1, 4, 0:P:GROUP],
                                          ALU.subtract).then_inc(att.log_scale, 1)
                        dve.tensor_tensor(rows[:, :, AW:ROW].rearrange("p s h -> p h s"), back,
                                          last_edge[:, bass.ds(slot, GROUP)].unsqueeze(1)
                                          .to_broadcast([P, HEADS, GROUP]), ALU.mult)
                        _, at = nc.values_load_multi_w_load_instructions(
                            offsets[0:1, bass.ds(slot, 1)], engines=[DVE_E], min_val=0, max_val=(NT - 1) * ROW,
                            skip_runtime_bounds_check_because=BOUNDED)
                        dve.wait_ge(att.scale, done + 1)
                        dve.wait_ge(att.added, FREE_BANKS + n * NS + slot)
                        first = acc[:, bass.ds(at[0], AW)].rearrange("p (h c) -> p h c", h=HEADS)
                        dve.tensor_tensor(first, first, old_scale[:, :].unsqueeze(2).to_broadcast([P, HEADS, HW]),
                                          ALU.mult).then_inc(att.used, 1)
                        dve.wait_ge(att.prob, done + 1)
                        for k in range(GROUP + LEAD):
                            if k < GROUP:
                                part_rows = rows[:, k, 0:AW].rearrange("p (h c) -> p h c", h=HEADS)
                                dve.tensor_tensor(part_rows, part_rows,
                                                  prob[:, :, k].unsqueeze(2).to_broadcast([P, HEADS, HW]),
                                                  ALU.mult).then_inc(att.weighted, 1)
                            if k == LEAD:
                                dve.wait_ge(att.used, done + 1 + FREE)
                                dve.sem_inc(dve_tick, 1)
                            if k >= LEAD:
                                add_sum(slot, 2 * GROUP + n * NS + slot, FREE_BANKS + n * NS + slot, k - LEAD)

                dve.wait_ge(att.added, FREE_BANKS + (n + 1) * NS)
                dve.wait_ge(att.dst_scored, (n + 1) * (NG + 1))
                with dve.Fori(0, NTG) as i:
                    k = n * 2 * NTG + i * 2
                    own = H[:, bass.ds(i * TG, TG), :]
                    sums = acc_t[:, bass.ds(i * TG, TG), :]
                    dve.tensor_tensor(selfs[:, 0, :, :], own[:, :, AW:ROW], score_t[:, bass.ds(i * TG, TG), :], ALU.add)
                    dve.tensor_tensor(selfs[:, 1, :, :], sums[:, :, AW:ROW],
                                      no_edge_far[:, bass.ds(i * TG, TG)].unsqueeze(2).to_broadcast([P, TG, HEADS]),
                                      ALU.add)
                    then()
                    dve.scalar_tensor_tensor(out=selfs[:, 2, :, :], in0=selfs[:, 0, :, :], scalar=SLOPE,
                                             in1=selfs[:, 0, :, :], op0=ALU.mult, op1=ALU.max)
                    then()
                    dve.tensor_tensor(selfs[:, 5, :, :], selfs[:, 1, :, :], selfs[:, 2, :, :], ALU.max)
                    then()
                    dve.tensor_tensor(selfs[:, 3:5, :, :], selfs[:, 1:3, :, :],
                                      selfs[:, 5, :, :].unsqueeze(1).to_broadcast([P, 2, TG, HEADS]),
                                      ALU.subtract).then_inc(n3.scored, 1)
                    dve.wait_ge(n3.weights, k + 1)

                    def heads(v):
                        return v[:, :, 0:AW].rearrange("p t (h c) -> p t h c", h=HEADS)

                    for v, w in ((sums, 3), (own, 4)):
                        dve.tensor_tensor(heads(v), heads(v),
                                          selfs[:, w, :, :].unsqueeze(3).to_broadcast([P, TG, HEADS, HW]), ALU.mult)
                    then()
                    dve.tensor_tensor(sums[:, :, 0:AW], sums[:, :, 0:AW], own[:, :, 0:AW], ALU.add)
                    then()
                    dve.reciprocal(selfs[:, 0, :, :], heads(sums)[:, :, :, HC])
                    then()
                    dve.tensor_tensor(xn[:, :, :].rearrange("p t (h c) -> p t h c", h=HEADS),
                                      heads(sums)[:, :, :, 0:HC],
                                      selfs[:, 0, :, :].unsqueeze(3).to_broadcast([P, TG, HEADS, HC]), ALU.mult)
                    then()
                    dve.tensor_tensor(xn[:, :, :], xn[:, :, :],
                                      att_bias[:, n, :].unsqueeze(1).to_broadcast([P, TG, D]), ALU.add)
                    then()
                    dve.tensor_scalar(sq[:, :, :], xn[:, :, :], 0.0, None, ALU.min).then_inc(n3.scored, 1)
                    dve.tensor_scalar(xc[:, :, :], xn[:, :, :], 0.0, 1.0, ALU.max, ALU.subtract)
                    then()
                    dve.wait_ge(n3.weights, k + 2)
                    if n < LAYERS - 1:
                        dve.tensor_tensor(xn[:, :, :], xc[:, :, :], sq[:, :, :], ALU.add).then_inc(n3.next, 1)
                        dve.wait_ge(n3.product, n * NTG + i + 1)
                        write_rows(i, n + 1).then_inc(n3.rows, 1)
                        then()
                    else:
                        x_group = X[:, bass.ds(i * TG, TG), :]
                        dve.tensor_tensor(x_group, x_group, xc[:, :, :], ALU.add)
                        then()
                        dve.tensor_tensor(x_group, x_group, sq[:, :, :], ALU.add)
                        then()
                        layer_norm(x_group, xn[:, :, :], n3, i + 1)
                        dve.wait_ge(n3.stats_gathered, 16 * NT)
                        dve.tensor_tensor(cat[:, :, 0:2 * EA], node_stats_in[:, bass.ds(i * TG, TG), :],
                                          has_edge[:, bass.ds(i * TG, TG)].unsqueeze(2)
                                          .to_broadcast([P, TG, 2 * EA]), ALU.mult)
                        then()
                        dve.tensor_tensor(cat[:, :, 2 * EA:3 * EA], cat[:, :, 0:EA],
                                          inv_degree[:, bass.ds(i * TG, TG)].unsqueeze(2)
                                          .to_broadcast([P, TG, EA]), ALU.mult).then_inc(n3.next, 1)
                        dve.tensor_tensor(x_group, x_group, xn[:, :, :], ALU.add)
                        then()
                        dve.wait_ge(n3.product, (LAYERS - 1) * NTG + i + 1)
                        dve.tensor_tensor(x_group, x_group, bank[:, 0:TG, 0:P], ALU.add).then_inc(n3.rows, 1)
                        then()


_ARGS = ["x", "chunks", "dst_line", "edge_attr", "w_self", "w_neigh", "b_neigh", "w_l", "w_r", "b_l", "gn_weight",
         "gn_bias", "mean_scale", "w_att", "att_src", "att_dst", "att_bias", "u", "w1", "b1", "w2", "b2"]


def kernel(x, src, dst, edge_attr_48, L0_gnn_w_self, L0_gnn_w_neigh, L0_gnn_b_neigh, L1_gnn_Wl, L1_gnn_bl,
           L1_gnn_Wr, L1_gnn_gn_weight, L1_gnn_gn_bias, L1_gnn_mean_scale, L2_gnn_W, L2_gnn_att_src,
           L2_gnn_att_dst, L2_gnn_bias, L3_gnn_u, L3_gnn_W1, L3_gnn_b1, L3_gnn_W2, L3_gnn_b2):
    import numpy as np
    import concourse.bacc as bacc
    from concourse.bass_utils import run_bass_kernel_spmd

    g = geometry(x.shape[0], src.shape[0])

    def padded(v, length, value):
        v = np.asarray(v)
        return np.concatenate([v, np.full((length - v.shape[0],) + v.shape[1:], value, v.dtype)])

    pad_node = g.tiles * P - 1
    src_p, dst_p = padded(src, g.rows * P, 0), padded(dst, g.rows * P, pad_node)
    chunks = np.zeros((g.rows, SD_W), np.int32)
    chunks[:, 0:P] = src_p.reshape(-1, P)
    chunks[:, P:2 * P] = dst_p.reshape(-1, P)
    chunks[:, 2 * P] = np.append(dst_p[P::P], np.int32(-1))
    arrays = {
        "x": padded(x, g.tiles * P, 0), "chunks": chunks,
        "dst_line": np.concatenate([np.full(1, -1, np.int32), dst_p]),
        "edge_attr": padded(edge_attr_48, g.rows * P, 0),
        "w_self": L0_gnn_w_self, "w_neigh": L0_gnn_w_neigh, "b_neigh": L0_gnn_b_neigh,
        "w_l": np.asarray(L1_gnn_Wl).T, "w_r": np.asarray(L1_gnn_Wr).T, "b_l": L1_gnn_bl,
        "gn_weight": L1_gnn_gn_weight, "gn_bias": L1_gnn_gn_bias, "mean_scale": L1_gnn_mean_scale,
        "w_att": L2_gnn_W, "att_src": L2_gnn_att_src, "att_dst": L2_gnn_att_dst, "att_bias": L2_gnn_bias,
        "u": L3_gnn_u, "w1": L3_gnn_W1, "b1": L3_gnn_b1, "w2": L3_gnn_W2, "b2": L3_gnn_b2,
    }
    nc = bacc.Bacc("TRN2", target_bir_lowering=False, num_devices=1)
    feeds, aps = {}, {}
    for name in _ARGS:
        v = np.ascontiguousarray(arrays[name])
        feeds[f"in_{name}"] = v
        aps[name] = nc.dram_tensor(f"in_{name}", v.shape, mybir.dt.from_np(v.dtype), kind="ExternalInput").ap()
    out = nc.dram_tensor("out_x", (g.tiles * P, D), F32, kind="ExternalOutput").ap()
    build_graph_network(nc, g, aps, out)
    r = run_bass_kernel_spmd(nc, [feeds], core_ids=[0])
    return r.results[0]["out_x"][:g.nodes]
```

```python
from collections import namedtuple
from contextlib import ExitStack

import concourse.bass as bass
from concourse import mybir

P = 128
D = 128
HEADS = 4
HC = D // HEADS
HW = HC + 1
AW = HEADS * HW
ROW = AW + HEADS
LAYERS = 3
EA = 48
UD = 16
HID = 256
ROUND = 8
GROUP = 32

TG = 7
SD_W = 2 * P + 4
EPS = 1e-5
SLOPE = 0.2
PARTS = 3
LEAD = 4
FAR = -1.0e30
EDGE_FAR = -3.0e38

F32 = mybir.dt.float32
I32 = mybir.dt.int32
BF16 = mybir.dt.bfloat16
ALU = mybir.AluOpType
ACT = mybir.ActivationFunctionType
AX = mybir.AxisListType
DVE_E = mybir.EngineType.DVE
PE_E = mybir.EngineType.PE
BOUNDED = "tile indices are clamped to the last tile when the table is made"


Geometry = namedtuple("Geometry", "nodes edges tiles chunks slots blocks rows groups")


def geometry(nodes, edges):
    tiles = -(-nodes // (P * TG)) * TG
    chunks = -(-edges // P)
    slots = -(-(chunks + tiles - 1) // (2 * GROUP)) * 2 * GROUP
    blocks = slots // P if slots % P == 0 else slots // P + 1
    return Geometry(nodes=nodes, edges=edges, tiles=tiles, chunks=chunks, slots=slots,
                    blocks=blocks, rows=blocks * P, groups=slots // GROUP)


def build_graph_network(nc, g, a, out):
    NT, NS, NB, NR, NG = g.tiles, g.slots, g.blocks, g.rows, g.groups
    NTG = NT // TG
    FREE_BANKS = 4
    FREE = 1

    table = nc.dram_tensor("row_table", [NT * P, ROW], F32).ap()
    slot_first = nc.dram_tensor("slot_first", [NR, 1], F32).ap()
    change_rows = nc.dram_tensor("change_rows", [NR, P + 1], F32).ap()
    dst_rows = nc.dram_tensor("dst_rows", [NR + GROUP, P], BF16).ap()
    slot_masks = nc.dram_tensor("slot_masks", [3, NR + GROUP], F32).ap()
    new_segment = nc.dram_tensor("new_segment", [NR * P], F32).ap()
    same_segment = nc.dram_tensor("same_segment", [NR * P], F32).ap()
    edge_stats = nc.dram_tensor("edge_stats", [NR * P, 2 * EA], F32).ap()

    with ExitStack() as ctx:
        def sb(name, shape, dt=F32):
            return ctx.enter_context(nc.sbuf_tensor(name, shape, dt))

        def sem(name):
            return ctx.enter_context(nc.semaphore(name))

        def sems(stage, names):
            return namedtuple(stage, names)(*[sem(f"{stage}_{n}") for n in names.split()])

        ctx.enter_context(nc.allow_non_contiguous_dma(reason="tables of indices, a few KB"))
        bank = ctx.enter_context(nc.psum_tensor("bank", [P, 8, 512], F32))

        X = sb("X", [P, NT, D])
        H = sb("H", [P, NT, ROW])
        acc = sb("acc", [P, NT * ROW])
        dst_local = sb("dst_local", [P, NR + 2 * GROUP])
        src_of = sb("src_of", [P, NR + 2 * GROUP])
        last_edge = sb("last_edge", [P, NR + 2 * GROUP], BF16)
        offsets = sb("offsets", [64, NR + 2 * GROUP], I32)
        dst_score = sb("dst_score", [P, NT * HEADS])
        dst_parts = sb("dst_parts", [P, NT * PARTS * HEADS], BF16)
        gathered = sb("gathered", [P, 2 * GROUP, ROW])
        pick = sb("pick", [P, GROUP, P])
        staged_idx = sb("staged_idx", [P, 2 * GROUP], I32)
        node_stat = sb("node_stat", [P, 6, NT])
        degree, inv_degree, has_edge, no_edge_far, real_node, rows_before = (
            node_stat[:, k, :] for k in range(6))
        last_row = sb("last_row", [P, NT], I32)

        ident = sb("ident", [P, P])
        col_index = sb("col_index", [P, P])
        tri = sb("tri", [P, P])
        tri_strict = sb("tri_strict", [P, P])
        ones = sb("ones", [P, P])
        part_index = sb("part_index", [P, 1])
        w_self = sb("w_self", [D, D])
        w_neigh = sb("w_neigh", [D, D])
        w_l = sb("w_l", [D, D])
        w_r = sb("w_r", [D, D])
        w_att = sb("w_att", [D, LAYERS, D + 2 * HEADS])
        att_vec = sb("att_vec", [D, LAYERS, 2 * HEADS])
        w1 = sb("w1", [P, 4, HID])
        w2 = sb("w2", [P, 2, D])
        bias_row = sb("bias_row", [1, D])
        node_bias = sb("node_bias", [P, 2, D])
        att_bias = sb("att_bias", [P, LAYERS, D])
        norm_par = sb("norm_par", [P, 3, D])
        u0 = sb("u0", [UD, 1])
        b1 = sb("b1", [P, 2])

        WEIGHTS = 2 * LAYERS * HEADS + 18 + LAYERS

        GW = TG * D
        scratch_mem = sb("scratch", [P, 6 * GW + 3 * TG * EA])

        def over(start, parts, *shape):
            size = 1
            for n in shape:
                size *= n
            v = scratch_mem[0:parts, start:start + size]
            return v.rearrange("p (a b) -> p a b", a=shape[0]) if len(shape) == 2 else v

        xc, sq, xn, tr_a, tr_b = (over(n * GW, P, TG, D) for n in range(5))
        tr_c = over(5 * GW, EA, TG, P)
        cat = over(6 * GW, P, TG, 3 * EA)
        ln_stats = sb("ln_stats", [P, TG, 6])
        ln_mean_var = sb("ln_mean_var", [P, TG, 2])
        ln_root = sb("ln_root", [P, 2, TG])
        ln_coef = sb("ln_coef", [P, 2, TG])
        rest = sb("rest", [P, TG, HEADS])

        minus_one = sb("minus_one", [P, 1])
        ea_in = scratch_mem[:, 0:2 * ROUND * EA].rearrange("p (b c w) -> p b c w", b=2, c=ROUND)
        ea_flag = over(2 * ROUND * EA, EA, 2, ROUND * P)
        ea_scan = over(2 * ROUND * (EA + P), EA, 1024)
        ea_out = over(2 * ROUND * (EA + P) + 1024, P, 2, ROUND * EA)
        start_flag = over(0, GROUP, 2, HEADS * P)
        end_flag = over(1024, GROUP, 2, HEADS * P)
        seg_f = over(2048, GROUP, 512)
        seg_m = over(2560, GROUP, 512)
        grp_sb = over(3072, GROUP, 512)
        raw, score, prob = (over(3584 + n * P, P, HEADS, GROUP) for n in range(3))
        masks = sb("masks", [HEADS, 2, 3, GROUP + 1])
        carry_f = sb("carry_f", [HEADS, GROUP + 1])
        carry_b = sb("carry_b", [HEADS, GROUP + 1])
        cross = sb("cross", [HEADS, 2, GROUP])
        pick_t = scratch_mem[:, 3968:3968 + GROUP * P // 2].bitcast(BF16).rearrange("p (k e) -> p k e", k=GROUP)
        pick_dist = sb("pick_dist", [P, ROUND, P], BF16)
        log_scale = sb("log_scale", [1, HEADS])
        old_scale = sb("old_scale", [P, HEADS])

        acc_f = acc[:, :]
        sd_row = acc_f[:, 0:NB * SD_W].bitcast(I32).rearrange("p (k c) -> p k c", k=NB)
        dst_row = acc_f[:, NB * SD_W:NB * (SD_W + P + 1)].rearrange("p (k c) -> p k c", k=NB)
        big = gathered[:, :, :].rearrange("p a b -> p (a b)")

        def part(n):
            return big[:, n * NB * P:(n + 1) * NB * P]

        first_row, scratch = part(0), part(1)
        diag = part(2).rearrange("p (k c) -> p k c", k=NB)
        edge_now, edge_before = (part(n).bitcast(I32).rearrange("p (k c) -> p k c", k=NB) for n in (3, 4))
        src_row, is_last = (part(n).rearrange("p (k c) -> p k c", k=NB) for n in (0, 2))
        change = big[:, 3 * NB * P:3 * NB * P + NB * (P + 1)].rearrange("p (k c) -> p k c", k=NB)
        pick_f = pick[:, :, :].rearrange("p a b -> p (a b)")
        flag_a = pick_f[:, 0:NB * P].rearrange("p (k c) -> p k c", k=NB)
        flag_b = pick_f[:, NB * P:2 * NB * P].rearrange("p (k c) -> p k c", k=NB)
        change_keep = pick_f[:, 0:NB * (P + 1)].rearrange("p (k c) -> p k c", k=NB)
        half = NB * (P + 1) + P
        dst_bf = pick_f[:, half:half + NB * P // 2].bitcast(BF16).rearrange("p (k c) -> p k c", k=NB)
        dst_tail = pick_f[0:GROUP, half + NB * P // 2:half + (NB + 1) * P // 2].bitcast(BF16)
        masks_row = scratch_mem[0:1, 0:3 * (NR + GROUP)].rearrange("p (m n) -> p m n", m=3)
        line_a, line_b, line_c, line_d = (acc[0:1, n * NR:(n + 1) * NR] for n in range(4))
        edge_cmp = part(1).bitcast(I32).rearrange("p (k c) -> p k c", k=NB)
        tile_cols = over(3 * (NR + GROUP), P, NB, 33)
        end_cols = sb("end_cols", [P, 2, NB])
        att_w = big[:, NT * 2 * EA:NT * (2 * EA + 6 * HEADS)].rearrange("p (m t h) -> p m t h", m=6, h=HEADS)
        STATS_FREE = GROUP * ROW // (2 * EA)
        x_flat = X[:, :, :].rearrange("p t d -> p (t d)")
        h_flat = H[:, :, :].rearrange("p t w -> p (t w)")
        xn_flat = xn[:, :, :].rearrange("p t d -> p (t d)")
        node_stats_in = big[:, 0:NT * 2 * EA].rearrange("p (t w) -> p t w", w=2 * EA)
        hid = pick_f[:, 0:2 * TG * P].rearrange("p (m n) -> p m n", m=2)
        cross_rows = sb("cross_rows", [GROUP, 2 * HEADS])
        iota_nodes = sb("iota_nodes", [P, NT], I32)
        pro = sb("pro", [P, 12, NB])
        (slot_no, chunk_tile, chunk_last, count, before, total, upto, slots_to, chunk_of, first_of, tile_of,
         tmp) = (pro[:, n, :] for n in range(12))
        chunk_idx = sb("chunk_idx", [P, NB], I32)
        int_tmp = sb("int_tmp", [P, NB, 2], I32)
        iota_i = sb("iota_i", [P, P], I32)
        iota_s = sb("iota_s", [P, 1 + NB], I32)

        acc_t = acc[:, :].rearrange("p (t w) -> p t w", w=ROW)
        parts_t = dst_parts[:, :].rearrange("p (t m h) -> p t m h", m=PARTS, h=HEADS)
        score_t = dst_score[:, :].rearrange("p (t h) -> p t h", h=HEADS)

        def flat(b):
            return bank[:, b:b + 2, :].rearrange("p a b -> p (a b)")[:, 0:TG * P]

        def cols(b, t):
            return bank[:, b + t // 4, (t % 4) * P:(t % 4 + 1) * P]

        def by_tile(v):
            return v.rearrange("p (t d) -> p t d", t=TG)

        rows_a = bank[:, 0:4, :].rearrange("p a b -> p (a b)")
        rows_b = bank[:, 4:8, :].rearrange("p a b -> p (a b)")

        pre = sems("pre", "x_loaded weights_loaded tables_loaded zeroed iota counted prefixed placed spread "
                          "firsts_stored dst_kept dst_stored indexed rows_gathered firsts_gathered split "
                          "turned_a copied_a turned_b copied_b edge_flags flags_stored changes changes_stored w_turned w_copied w_made w_kept "
                          "ends_turned masks_ready masks_stored tail_zeroed")
        tick = sem("pool_tick")
        pe_tick = sem("tensor_tick")
        dve_tick = sem("vector_tick")
        act_tick = sem("scalar_tick")
        table_stored = sem("table_stored")
        ln = sems("ln", "var root coef normed")
        tab = sems("tab", "turned copied product rows parts")
        n1 = sems("n1", "degrees inverted prefixed prefix_used scaled turned copied product taken joined")
        n2 = sems("n2", "rows scaled turned copied product gelu joined gathered_sums colsum centred squares "
                        "summed colvar colroot norm_ready x_done")
        n3 = sems("n3", "scored weights weighed own_ready summed joined elu next turned copied hidden relu "
                        "product added stats_gathered stored")
        mean = sems("mean", "staged gathered0 gathered1 gathered2 gathered3 picked loaded0 loaded1 turned "
                            "scanned turned_back copied stored0 stored1 summed added")
        att = sems("att", "staged picked rows_loaded turned dst_scored summed added flags0 flags1 "
                          "scored score_rows firsts ends crossed cross_rows maxima max_back shifted prob "
                          "log_scale scale_rows scale weighted used")
        att_gathered = [[sem(f"att{n}_gathered{b}") for b in range(2)] for n in range(LAYERS)]
        mean_gathered = [mean.gathered0, mean.gathered1, mean.gathered2, mean.gathered3]
        mean_loaded = [mean.loaded0, mean.loaded1]
        mean_stored = [mean.stored0, mean.stored1]
        att_flags = [att.flags0, att.flags1]
        RNG = GROUP // ROUND
        ROUNDS = NS // ROUND
        PAIRS = NG // 2
        MEAN_W = D + 1
        QG = GROUP // 4

        block = ctx.enter_context(nc.Block())

        def over_groups(eng, steps):
            def run(i):
                for step, by in steps:
                    if not isinstance(i, int) or 0 <= i + by < NTG:
                        step(i + by)

            ahead = max(by for _, by in steps)
            for i in range(-ahead, 0):
                run(i)
            if NTG > ahead:
                with eng.Fori(0, NTG - ahead) as i:
                    run(i)
            for i in range(max(NTG - ahead, 0), NTG):
                run(i)

        @block.sync
        def _(sp):
            sp.dma_start(X[:, :, :], a["x"].rearrange("(t p) d -> p t d", p=P)).then_inc(pre.x_loaded, 16)
            sp.dma_start(edge_now, a["dst_line"][1:1 + NR * P].rearrange("(k q e) -> q k e", q=P, e=P)
                         ).then_inc(pre.tables_loaded, 16)
            sp.dma_start(edge_before, a["dst_line"][0:NR * P].rearrange("(k q e) -> q k e", q=P, e=P)
                         ).then_inc(pre.tables_loaded, 16)
            sp.wait_ge(pre.zeroed, 1)
            weights = 0
            for n in range(LAYERS):
                for h in range(HEADS):
                    for v, name in enumerate(("att_src", "att_dst")):
                        sp.dma_start(att_vec[h * HC:(h + 1) * HC, n, v * HEADS + h:v * HEADS + h + 1],
                                     a[name][n, h, :].unsqueeze(1)).then_inc(pre.weights_loaded, 16)
                        weights += 1
            for dst, src in ((w_self[:, :], a["w_self"]), (w_neigh[:, :], a["w_neigh"]),
                             (w_l[:, :], a["w_l"]), (w_r[:, :], a["w_r"]),
                             (w_att[:, :, 0:D], a["w_att"].rearrange("l k n -> k l n")),
                             (w1[:, 0, :], a["w1"][0:D, :]),
                             (w1[0:2 * EA, 1, :], a["w1"][D:D + 2 * EA, :]),
                             (w1[0:EA, 2, :], a["w1"][D + 2 * EA:D + 3 * EA, :]),
                             (w1[0:UD, 3, :], a["w1"][D + 3 * EA:D + 3 * EA + UD, :]),
                             (w2[:, :, :], a["w2"].rearrange("(m k) n -> k m n", k=P)),
                             (bias_row[:, :], a["b_l"].unsqueeze(0)),
                             (node_bias[:, 0, :], a["b_neigh"].unsqueeze(0).to_broadcast([P, D])),
                             (node_bias[:, 1, :], a["b2"].unsqueeze(0).to_broadcast([P, D])),
                             (u0[:, :], a["u"][0, :].unsqueeze(1)),
                             (b1[:, :], a["b1"].rearrange("(m k) -> k m", k=P)),
                             (norm_par[:, 0, :], a["gn_weight"].unsqueeze(0).to_broadcast([P, D])),
                             (norm_par[:, 1, :], a["gn_bias"].unsqueeze(0).to_broadcast([P, D])),
                             (norm_par[:, 2, :], a["mean_scale"].unsqueeze(0).to_broadcast([P, D]))):
                sp.dma_start(dst, src).then_inc(pre.weights_loaded, 16)
                weights += 1
            for n in range(LAYERS):
                sp.dma_start(att_bias[:, n, :], a["att_bias"][n, :].unsqueeze(0).to_broadcast([P, D])
                             ).then_inc(pre.weights_loaded, 16)
                weights += 1
            assert weights == WEIGHTS

            def store_rows(i):
                sp.dma_start(table.rearrange("(t p) w -> p t w", p=P)[:, bass.ds(i * TG, TG), :],
                             H[:, bass.ds(i * TG, TG), :]).then_inc(table_stored, 16)

            sp.wait_ge(pre.placed, 1)
            sp.dma_start(slot_first.rearrange("(k q) o -> q (k o)", q=P), before).then_inc(pre.firsts_stored, 16)
            sp.wait_ge(pre.edge_flags, 1)
            sp.dma_start(new_segment.rearrange("(k q e) -> q k e", q=P, e=P), flag_a).then_inc(pre.flags_stored, 16)
            sp.dma_start(same_segment.rearrange("(k q e) -> q k e", q=P, e=P), flag_b).then_inc(pre.flags_stored, 16)
            with sp.Fori(0, NTG) as i:
                sp.wait_ge(ln.normed, i + 1 + FREE)
                store_rows(i)
            sp.wait_ge(pre.changes, 1)
            sp.dma_start(change_rows.rearrange("(k q) e -> q k e", q=P), change_keep
                         ).then_inc(pre.changes_stored, 16)
            sp.wait_ge(pre.dst_kept, 1)
            sp.dma_start(dst_rows[0:NR, :].rearrange("(k q) e -> q k e", q=P), dst_bf).then_inc(pre.dst_stored, 16)
            sp.dma_start(dst_rows[NR:NR + GROUP, :], dst_tail).then_inc(pre.dst_stored, 16)


            def mean_loads(n):
                with sp.Fori(0, NG) as it:
                    for q in range(RNG):
                        base = n * ROUNDS
                        b = q % 2
                        if q < 2:
                            sp.wait_ge(mean.scanned, base + it * RNG + q + FREE)
                        else:
                            sp.wait_ge(mean.scanned, base + it * RNG + q - 1 + FREE)
                        at = it * (GROUP * P) + q * ROUND * P
                        sp.dma_start(ea_in[:, b, :, :],
                                     a["edge_attr"].rearrange("(c e) w -> e c w", e=P)[
                                         :, bass.ds(it * GROUP + q * ROUND, ROUND), :]).then_inc(mean_loaded[b], 16)
                        flags = new_segment if n == 0 else same_segment
                        sp.dma_start(ea_flag[:, b, :],
                                     flags[bass.ds(at, ROUND * P)].unsqueeze(0).to_broadcast([EA, ROUND * P])
                                     ).then_inc(mean_loaded[b], 16)

            sp.wait_ge(pre.flags_stored, 32)
            sp.wait_ge(pre.w_made, LAYERS + 2)
            mean_loads(0)
            with sp.Fori(0, NTG) as i:
                sp.wait_ge(ln.normed, NTG + i + 1 + FREE)
                store_rows(i)
            sp.wait_ge(pre.masks_ready, 1)
            sp.dma_start(slot_masks.unsqueeze(0), masks_row).then_inc(pre.masks_stored, 16)
            sp.wait_ge(pre.masks_stored, 16)
            mean_loads(1)
            with sp.Fori(0, NTG) as i:
                sp.wait_ge(tab.rows, 0 * NTG + i + 1 + FREE)
                sp.wait_ge(tab.parts, 0 * NTG + i + 1 + FREE)
                store_rows(i)
            sp.wait_ge(pre.changes_stored, 16)
            sp.wait_ge(pre.masks_stored, 16)
            sp.wait_ge(pre.dst_stored, 32)

            def load_dst(slot):
                sp.dma_start(pick_t, dst_rows[bass.ds(slot, GROUP), :].unsqueeze(0).to_broadcast([P, GROUP, P])
                             ).then_inc(att.rows_loaded, 16)

            sp.sem_inc(att.used, FREE)
            for n in range(LAYERS):
                load_dst(0)
                with sp.Fori(0, PAIRS) as it:
                    for b in range(2):
                        sp.wait_ge(att.used, n * NG + it * 2 + b + FREE)
                        slot = it * (2 * GROUP) + b * GROUP
                        for view, col in ((start_flag, 0), (end_flag, 1)):
                            sp.dma_start(view[:, b, :].rearrange("s (h e) -> s h e", h=HEADS),
                                         change_rows[bass.ds(slot, GROUP), col:col + P].unsqueeze(1)
                                         .to_broadcast([GROUP, HEADS, P])).then_inc(att_flags[b], 16)
                        sp.dma_start(masks[:, b, :, :],
                                     slot_masks[:, bass.ds(slot, GROUP + 1)].unsqueeze(0)
                                     .to_broadcast([HEADS, 3, GROUP + 1])).then_inc(att_flags[b], 16)
                        sp.wait_ge(att.dst_scored, n * (NG + 1) + it * 2 + b + 1)
                        load_dst(slot + GROUP)
                if n < LAYERS - 1:
                    with sp.Fori(0, NTG) as i:
                        sp.wait_ge(tab.rows, (n + 1) * NTG + i + 1 + FREE)
                        sp.wait_ge(tab.parts, (n + 1) * NTG + i + 1 + FREE)
                        store_rows(i)
            with sp.Fori(0, NTG) as i:
                sp.wait_ge(n3.added, i + 1 + FREE)
                sp.dma_start(out.rearrange("(t p) w -> p t w", p=P)[:, bass.ds(i * TG, TG), :],
                             X[:, bass.ds(i * TG, TG), :]).then_inc(n3.stored, 16)
            sp.wait_ge(n3.stored, 16 * NTG)

        @block.gpsimd
        def _(pool):
            pool.memset(att_vec[:, :, :], 0.0).then_inc(pre.zeroed, 1)
            pool.iota(iota_i[:, :], pattern=[[1, P]], base=0, channel_multiplier=0).then_inc(pre.iota, 1)
            pool.iota(iota_s[:, 0:1], pattern=[[0, 1]], base=0, channel_multiplier=1).then_inc(pre.iota, 1)
            pool.iota(iota_s[:, 1:1 + NB], pattern=[[P, NB]], base=0, channel_multiplier=1).then_inc(pre.iota, 1)
            pool.iota(iota_nodes[:, :], pattern=[[P, NT]], base=0, channel_multiplier=1).then_inc(pre.iota, 1)
            pool.wait_ge(pre.firsts_stored, 16)
            pool.wait_ge(pre.indexed, 1)
            for k in range(NB):
                pool.indirect_dma_start(sd_row[:, k, :], None, a["chunks"],
                                        bass.IndirectOffsetOnAxis(chunk_idx[:, k:k + 1], 0)
                                        ).then_inc(pre.rows_gathered, 16)
            for k in range(NB):
                pool.indirect_dma_start(first_of[:, k:k + 1], None, slot_first,
                                        bass.IndirectOffsetOnAxis(chunk_idx[:, k:k + 1], 0)
                                        ).then_inc(pre.firsts_gathered, 16)

            def own_rows(eng, n, i):
                eng.tensor_tensor(xc[:, :, :].rearrange("p t (h c) -> p t h c", h=HEADS),
                                  H[:, bass.ds(i * TG, TG), 0:AW].rearrange("p t (h c) -> p t h c",
                                                                            h=HEADS)[:, :, :, 0:HC],
                                  att_w[:, 5, bass.ds(i * TG, TG), :].unsqueeze(3).to_broadcast([P, TG, HEADS, HC]),
                                  ALU.mult)
                eng.drain()
                return eng.tensor_tensor(xc[:, :, :], xc[:, :, :],
                                         att_bias[:, n, :].unsqueeze(1).to_broadcast([P, TG, D]), ALU.add)

            def mean_gathers(n):
                with pool.Fori(0, NG) as it:
                    for q in range(RNG):
                        pool.wait_ge(mean.staged, n * (ROUNDS + RNG - 1) + it * RNG + q + 1)
                        pool.sem_inc(tick, 1)
                        for k in range(q * ROUND, (q + 1) * ROUND):
                            pool.indirect_dma_start(gathered[:, k, :], None, table,
                                                    bass.IndirectOffsetOnAxis(staged_idx[:, k:k + 1], 0)
                                                    ).then_inc(mean_gathered[q], 16)

            def scale_sums(s, i, rows_too):
                pool.wait_ge(s.turned, 2 * i + FREE)
                pool.sem_inc(tick, 1)
                if rows_too:
                    pool.tensor_copy(xn[:, :, :], H[:, bass.ds(i * TG, TG), 0:D])
                pool.tensor_tensor(sq[:, :, :], acc_t[:, bass.ds(i * TG, TG), 0:D],
                                   inv_degree[:, bass.ds(i * TG, TG)].unsqueeze(2).to_broadcast([P, TG, D]),
                                   ALU.mult).then_inc(s.scaled, 1)

            pool.wait_ge(table_stored, 16 * NTG)
            pool.wait_ge(pre.copied_b, 2)
            mean_gathers(0)
            pool.wait_ge(n1.inverted, 1)
            pool.sem_inc(n1.turned, FREE)
            with pool.Fori(0, NTG) as i:
                scale_sums(n1, i, True)
                x_group = X[:, bass.ds(i * TG, TG), :]
                pool.tensor_tensor(x_group, x_group, node_bias[:, 0, :].unsqueeze(1).to_broadcast([P, TG, D]),
                                   ALU.add).then_inc(n1.joined, 1)
            pool.wait_ge(table_stored, 2 * 16 * NTG)
            mean_gathers(1)
            pool.wait_ge(mean.added, FREE_BANKS + 2 * NS)
            pool.sem_inc(n2.turned, FREE)
            with pool.Fori(0, NTG) as i:
                scale_sums(n2, i, False)
                x_group = X[:, bass.ds(i * TG, TG), :]
                pool.tensor_tensor(x_group, x_group, H[:, bass.ds(i * TG, TG), 0:D], ALU.add)
                pool.drain()
                pool.tensor_tensor(x_group, x_group, norm_par[:, 1, :].unsqueeze(1).to_broadcast([P, TG, D]),
                                   ALU.add).then_inc(n2.joined, 1)
            pool.wait_ge(n2.norm_ready, 1)
            with pool.Fori(0, NTG) as i:
                x_group = X[:, bass.ds(i * TG, TG), :]
                out_group = acc_t[:, bass.ds(i * TG, TG), 0:D]
                pool.tensor_tensor(out_group, out_group, tr_b[:, 0, :].unsqueeze(1).to_broadcast([P, TG, D]),
                                   ALU.mult)
                pool.drain()
                pool.tensor_tensor(x_group, x_group, out_group, ALU.add).then_inc(n2.x_done, 1)
            for n in range(LAYERS):
                pool.wait_ge(table_stored, (n + 3) * 16 * NTG)
                if n == 0:
                    pool.sem_inc(att.summed, 2 * GROUP)
                with pool.Fori(0, PAIRS) as it:
                    for b in range(2):
                        pool.wait_ge(att.staged, n * (NG + 2) + it * 2 + b + 1)
                        for q in range(RNG):
                            pool.wait_ge(att.summed, n * NS + it * (2 * GROUP) + b * GROUP + (q + 1) * ROUND)
                            pool.sem_inc(tick, 1)
                            for k in range(q * ROUND, (q + 1) * ROUND):
                                at = b * GROUP + k
                                pool.indirect_dma_start(gathered[:, at, :], None, table,
                                                        bass.IndirectOffsetOnAxis(staged_idx[:, at:at + 1], 0)
                                                        ).then_inc(att_gathered[n][b], 16)
                if n < LAYERS - 1:
                    if n == 0:
                        pool.sem_inc(n3.summed, FREE)
                    pool.wait_ge(n3.weighed, n + 1)
                    with pool.Fori(0, NTG) as i:
                        pool.wait_ge(n3.summed, n * NTG + i + FREE)
                        pool.sem_inc(tick, 1)
                        own_rows(pool, n, i).then_inc(n3.own_ready, 1)
            pool.wait_ge(mean_stored[0], 16 * (ROUNDS + FREE))
            pool.wait_ge(mean_stored[1], 16 * (ROUNDS + FREE))
            pool.wait_ge(att.summed, 2 * GROUP + LAYERS * NS - GROUP)
            pool.sem_inc(tick, 1)
            for t in range(NT):
                if t == STATS_FREE:
                    pool.wait_ge(att.summed, 2 * GROUP + LAYERS * NS)
                    pool.sem_inc(tick, 1)
                pool.indirect_dma_start(node_stats_in[:, t, :], None, edge_stats,
                                        bass.IndirectOffsetOnAxis(last_row[:, t:t + 1], 0)
                                        ).then_inc(n3.stats_gathered, 16)

        @block.scalar
        def _(act):
            def root(i, base):
                act.wait_ge(ln.var, base + i + 1)
                nc.scalar.activation(ln_root[:, 1, :], ln_root[:, 0, :], ACT.Sqrt).then_inc(ln.root, 1)

            def normalise(i, base, out):
                act.wait_ge(ln.coef, base + i + 1)
                act.sem_inc(act_tick, 1)
                for t in range(TG):
                    done = nc.scalar.activation(out(t), x_flat[:, bass.ds(i * (TG * D) + t * D, D)], ACT.Relu,
                                                scale=ln_coef[:, 0, t:t + 1], bias=ln_coef[:, 1, t:t + 1])
                done.then_inc(ln.normed, 1)

            def to_table(i):
                return lambda t: h_flat[:, bass.ds(i * (TG * ROW) + t * ROW, D)]

            def to_xn(t):
                return xn_flat[:, t * D:(t + 1) * D]

            def keep_turned(s, i):
                act.wait_ge(s.turned, 2 * i + 1 + FREE)
                nc.scalar.copy(tr_a[:, :, :], by_tile(flat(0))).then_inc(s.copied, 1)
                act.wait_ge(s.turned, 2 * i + 2 + FREE)
                nc.scalar.copy(tr_b[:, :, :], by_tile(flat(2))).then_inc(s.copied, 1)

            def table_out(k, i):
                act.wait_ge(tab.product, k * NTG + i + 1)
                act.sem_inc(act_tick, 1)
                nc.scalar.copy(H[:, bass.ds(i * TG, TG), 0:AW].rearrange("p t (h c) -> p t h c",
                                                                         h=HEADS)[:, :, :, 0:HC],
                               flat(2).rearrange("p (t h c) -> p t h c", t=TG, h=HEADS)).then_inc(tab.rows, 1)

            def table_turned(k, i):
                act.wait_ge(tab.turned, k * NTG + i + 1)
                if k == 0:
                    nc.scalar.copy(tr_a[:, :, :], by_tile(flat(0))).then_inc(tab.copied, 1)
                else:
                    nc.scalar.activation(tr_a[:, :, :], by_tile(flat(0)), ACT.Identity,
                                         bias=minus_one[:, 0:1]).then_inc(tab.copied, 1)

            def table_stage(k, first):
                over_groups(act, ((first, 2), (lambda i: table_out(k, i), 0), (lambda i: table_turned(k, i), 1)))

            with act.Fori(0, NTG) as i:
                root(i, 0)
                normalise(i, 0, to_table(i))
            act.wait_ge(pre.turned_a, 2 * NB)
            nc.scalar.copy(dst_local[:, 0:NR], rows_a[:, 0:NR]).then_inc(pre.copied_a, 1)
            nc.scalar.copy(src_of[:, 0:NR], rows_b[:, 0:NR]).then_inc(pre.copied_a, 1)

            def stage(n, r, q):
                nc.scalar.copy(staged_idx[:, q * ROUND:(q + 1) * ROUND],
                               src_of[:, bass.ds(r * ROUND, ROUND)] if not isinstance(r, int) else
                               src_of[:, r * ROUND:(r + 1) * ROUND]).then_inc(mean.staged, 1)

            def mean_scalar(n):
                if n == 0:
                    act.wait_ge(pre.tail_zeroed, 1)
                    act.wait_ge(pre.copied_a, 2)
                    act.sem_inc(mean.summed, FREE)
                    for stored in mean_stored:
                        act.sem_inc(stored, 16 * FREE)
                for r in range(RNG - 1):
                    stage(n, r, r)
                with act.Fori(0, NG) as it:
                    for q in range(RNG):
                        b = q % 2
                        act.wait_ge(mean.summed, n * NS + it * GROUP + q * ROUND + FREE)
                        stage(n, it * RNG + q + RNG - 1, (q + RNG - 1) % RNG)
                        act.wait_ge(mean.turned_back, n * ROUNDS + it * RNG + q + 1 + FREE)
                        act.wait_ge(mean_stored[b], 16 * (n * (ROUNDS // 2) + q // 2 + FREE) + it * (16 * RNG // 2))
                        nc.scalar.copy(ea_out[:, b, :], bank[:, 2 + b, 0:ROUND * EA]).then_inc(mean.copied, 1)
                        act.wait_ge(mean.copied, n * ROUNDS + it * RNG + q + 1 + FREE)
                        col = EA if n == 0 else 0
                        act.dma_start(edge_stats.rearrange("(c e) w -> e c w", e=P)[
                            :, bass.ds(it * GROUP + q * ROUND, ROUND), col:col + EA],
                            ea_out[:, b, :].rearrange("p (c w) -> p c w", w=EA)).then_inc(mean_stored[b], 16)

            def stores_landed(eng, n):
                for b in range(2):
                    eng.wait_ge(mean_stored[b], 16 * ((n + 1) * (ROUNDS // 2) + FREE))

            mean_scalar(0)
            stores_landed(act, 0)
            keep_turned(n1, 0)
            with act.Fori(0, NTG - 1) as i:
                keep_turned(n1, i + 1)
                root(i, NTG)
                normalise(i, NTG, to_table(i))
            root(NTG - 1, NTG)
            normalise(NTG - 1, NTG, to_table(NTG - 1))
            mean_scalar(1)
            stores_landed(act, 1)

            def gelu(i):
                act.wait_ge(n2.product, i + 1)
                act.sem_inc(act_tick, 1)
                nc.scalar.activation(acc_t[:, bass.ds(i * TG, TG), 0:D], by_tile(flat(4)), ACT.Gelu
                                     ).then_inc(n2.gelu, 1)

            with act.Fori(0, NTG) as i:
                gelu(i)
            act.sem_inc(n2.summed, FREE)
            with act.Fori(0, NTG) as i:
                act.wait_ge(n2.centred, i + 1)
                act.wait_ge(n2.summed, i + FREE)
                act.sem_inc(act_tick, 1)
                nc.scalar.activation(tr_a[:, :, :], acc_t[:, bass.ds(i * TG, TG), 0:D], ACT.Square
                                     ).then_inc(n2.squares, 1)

            act.wait_ge(n2.colvar, 1)
            nc.scalar.activation(tr_b[:, 3, :], tr_b[:, 1, :], ACT.Sqrt).then_inc(n2.colroot, 1)

            def normalise_next(i):
                root(i, 2 * NTG)
                if not (isinstance(i, int) and i == 0):
                    act.wait_ge(tab.turned, i)
                normalise(i, 2 * NTG, to_xn)

            table_stage(0, normalise_next)

            def act_picks(where, slot):
                for k in range(ROUND):
                    nc.scalar.activation(pick_dist[:, k, :], col_index[:, :], ACT.Abs, scale=-1.0,
                                         bias=dst_local[:, bass.ds(slot + k, 1)])
                act.drain()
                nc.scalar.activation(pick[:, where:where + ROUND, :], pick_dist[:, :, :], ACT.Relu, scale=-1.0,
                                     bias=ones[:, 0:1]).then_inc(att.picked, 1)
                act.drain()

            for n in range(LAYERS):
                for b in range(2):
                    nc.scalar.copy(staged_idx[:, b * GROUP:(b + 1) * GROUP],
                                   src_of[:, b * GROUP:(b + 1) * GROUP]).then_inc(att.staged, 1)

                for q in range(RNG):
                    act_picks(q * ROUND, q * ROUND)
                with act.Fori(0, PAIRS) as it:
                    for b in range(2):
                        act.wait_ge(att_gathered[n][b], 16 * GROUP + it * (16 * GROUP))
                        nc.scalar.copy(staged_idx[:, b * GROUP:(b + 1) * GROUP],
                                       src_of[:, bass.ds(it * (2 * GROUP) + (b + 2) * GROUP, GROUP)]
                                       ).then_inc(att.staged, 1)
                        act.wait_ge(att.shifted, n * NG + it * 2 + b + 1)
                        nc.scalar.activation(prob[:, :, :], score[:, :, :], ACT.Exp).then_inc(att.prob, 1)
                        act.wait_ge(att.scale_rows, n * NG + it * 2 + b + 1)
                        nc.scalar.activation(old_scale[:, :], bank[:, 5, 128:128 + HEADS], ACT.Exp
                                             ).then_inc(att.scale, 1)
                        slot = it * (2 * GROUP) + (b + 1) * GROUP
                        for q in range(RNG):
                            act.wait_ge(att.summed, 2 * GROUP + n * NS + slot - GROUP + (q + 1) * ROUND)
                            act_picks(q * ROUND, slot + q * ROUND)
                act.wait_ge(n3.scored, n + 1)
                nc.scalar.activation(att_w[:, 2:4, :, :], att_w[:, 2:4, :, :], ACT.Exp).then_inc(n3.weights, 1)
                if n == 0:
                    act.sem_inc(n3.elu, FREE)

                def exp_min(i):
                    act.wait_ge(n3.summed, n * NTG + i + 1 + FREE)
                    act.wait_ge(n3.elu, n * NTG + i + FREE)
                    act.sem_inc(act_tick, 1)
                    nc.scalar.activation(sq[:, :, :], H[:, bass.ds(i * TG, TG), 0:D], ACT.Relu, scale=-1.0)
                    act.drain()
                    nc.scalar.activation(sq[:, :, :], sq[:, :, :], ACT.Exp, scale=-1.0).then_inc(n3.weights, 1)

                if n < LAYERS - 1:
                    table_stage(n + 1, exp_min)

            def normalise_last(i):
                if not (isinstance(i, int) and i == 0):
                    act.wait_ge(n3.turned, 3 * i)
                    act.wait_ge(n3.joined, i)
                normalise(i, 3 * NTG, to_xn)

            def mlp(i):
                act.wait_ge(n3.turned, 3 * i + 1)
                nc.scalar.copy(tr_c[:, :, :], by_tile(flat(4))[0:EA])
                act.wait_ge(n3.turned, 3 * i + 2)
                nc.scalar.copy(tr_b[0:2 * EA, :, :], by_tile(flat(2))[0:2 * EA])
                act.wait_ge(n3.turned, 3 * i + 3)
                nc.scalar.copy(tr_a[:, :, :], by_tile(flat(0))).then_inc(n3.copied, 1)

            def mlp_relu(i):
                for m in range(2):
                    act.wait_ge(n3.hidden, i * 2 + m + 1)
                    b = 6 * (1 - m)
                    nc.scalar.activation(hid[:, m, :].rearrange("p (c n) -> p c n", c=2),
                                         bank[:, b:b + 2, 0:TG * P // 2], ACT.Relu,
                                         bias=b1[:, m:m + 1]).then_inc(n3.relu, 1)

            over_groups(act, ((mlp, 0), (exp_min, 1), (lambda i: root(i, 3 * NTG), 1), (mlp_relu, 0),
                              (normalise_last, 1)))

        @block.tensor
        def _(pe):
            pe.wait_ge(pre.counted, 1)
            pe.matmul(bank[:, 0, 0:NB], tri_strict[:, :], count, start=True, stop=True)
            pe.matmul(bank[:, 1, 0:NB], ones[:, :], count, start=True, stop=True).then_inc(pre.prefixed, 1)
            pe.wait_ge(pre.placed, 2)
            for k in range(NB):
                pe.matmul(rows_b[:, k * P:(k + 1) * P], ones[:, :], diag[:, k, :],
                          start=True, stop=True).then_inc(pre.spread, 1)
            pe.wait_ge(pre.split, 1)
            for k in range(NB):
                pe.transpose(rows_a[:, k * P:(k + 1) * P], dst_row[:, k, 0:P], ident[:, :]).then_inc(pre.turned_a, 1)
                pe.transpose(rows_b[:, k * P:(k + 1) * P], src_row[:, k, :], ident[:, :]).then_inc(pre.turned_a, 1)
            pe.wait_ge(pre.copied_a, 2)
            for k in range(NB):
                pe.transpose(rows_a[:, k * P:(k + 1) * P], is_last[:, k, :], ident[:, :]).then_inc(pre.turned_b, 1)
            for k in range(NB):
                pe.matmul(rows_b[0:33, k * P:(k + 1) * P], tile_cols[:, k, :], ident[:, :],
                          start=True, stop=True).then_inc(pre.turned_b, 1)
            pe.wait_ge(pre.copied_b, 2)
            pe.wait_ge(pre.weights_loaded, 16 * WEIGHTS)
            for n in range(LAYERS):
                pe.transpose(bank[:, n, 0:P], w_att[:, n, 0:D], ident[:, :]).then_inc(pre.w_turned, 1)
            pe.wait_ge(pre.w_copied, 1)
            for n in range(LAYERS):
                pe.matmul(bank[:, 4 + n, 0:2 * HEADS], pick[:, 24 + n, :], att_vec[:, n, :],
                          start=True, stop=True).then_inc(pre.w_made, 1)
            for m in range(2):
                pe.matmul(bank[:, 7, m:m + 1], w1[0:UD, 3, m * P:(m + 1) * P], u0[:, :],
                          start=True, stop=True).then_inc(pre.w_made, 1)
            pe.wait_ge(pre.w_kept, 1)

            def mean_tensor(n):
                if n == 0:
                    pe.sem_inc(mean.added, FREE_BANKS)
                    pe.sem_inc(mean.scanned, FREE)
                    pe.sem_inc(mean.copied, FREE)
                with pe.Fori(0, NG) as it:
                    for q in range(RNG):
                        b = q % 2
                        r = n * ROUNDS + q
                        pe.wait_ge(mean_loaded[b], 32 * (n * (ROUNDS // 2) + q // 2 + 1) + it * (32 * RNG // 2))
                        pe.wait_ge(mean.scanned, it * RNG + r + FREE)
                        pe.sem_inc(pe_tick, 1)
                        for c in range(ROUND):
                            mm = pe.transpose(bank[0:EA, c // 4, (c % 4) * P:(c % 4 + 1) * P], ea_in[:, b, c, :],
                                              ident[:, :])
                        mm.then_inc(mean.turned, 1)
                        pe.wait_ge(mean_gathered[q], 16 * ROUND * (n * NG + 1) + it * (16 * ROUND))
                        pe.wait_ge(mean.picked, it * RNG + r + 1)
                        for c in range(ROUND):
                            k = q * ROUND + c
                            pe.wait_ge(mean.added, n * NS + it * GROUP + k + 1)
                            pe.matmul(bank[:, 4 + k % 4, 0:MEAN_W], pick[:, k, :], gathered[:, k, 0:MEAN_W],
                                      start=True, stop=True).then_inc(mean.summed, 1)
                        pe.wait_ge(mean.scanned, it * RNG + r + 1 + FREE)
                        pe.wait_ge(mean.copied, it * RNG + r + FREE)
                        pe.sem_inc(pe_tick, 1)
                        for c in range(ROUND):
                            mm = pe.transpose(bank[:, 2 + b, c * EA:(c + 1) * EA], ea_scan[:, c * P:(c + 1) * P],
                                              ident[0:EA, 0:EA])
                        mm.then_inc(mean.turned_back, 1)

            mean_tensor(0)
            pe.wait_ge(n1.degrees, 1)
            pe.matmul(bank[:, 7, 0:NT], tri[:, :], degree, start=True, stop=True)
            pe.matmul(bank[:, 7, 64:64 + NT], ones[:, :], degree, start=True, stop=True).then_inc(n1.prefixed, 1)

            def banks_left(n):
                pe.wait_ge(mean.copied, (n + 1) * ROUNDS + FREE)
                pe.wait_ge(mean.added, FREE_BANKS + (n + 1) * NS)

            banks_left(0)

            def turn_two(s, i, rows_ready):
                pe.wait_ge(rows_ready, i + 1)
                for t in range(TG):
                    mm = pe.transpose(cols(0, t), xn[:, t, :], ident[:, :])
                mm.then_inc(s.turned, 1)
                pe.wait_ge(s.scaled, i + 1)
                for t in range(TG):
                    mm = pe.transpose(cols(2, t), sq[:, t, :], ident[:, :])
                mm.then_inc(s.turned, 1)

            def two_products(s, i, taken, w_own, w_mean, bias):
                pe.wait_ge(s.copied, 2 * i + 2)
                pe.wait_ge(taken, i + FREE)
                for t in range(TG):
                    pe.matmul(cols(4, t), tr_a[:, t, :], w_own, start=True, stop=False)
                    mm = pe.matmul(cols(4, t), tr_b[:, t, :], w_mean, start=False, stop=bias is None)
                    if bias is not None:
                        mm = pe.matmul(cols(4, t), ones[0:1, :], bias, start=False, stop=True)
                mm.then_inc(s.product, 1)

            pe.sem_inc(n1.taken, FREE)
            with pe.Fori(0, NTG) as i:
                turn_two(n1, i, n1.scaled)
                two_products(n1, i, n1.taken, w_self[:, :], w_neigh[:, :], None)
            pe.wait_ge(n1.prefix_used, 1)
            for k in range(NB):
                pe.matmul(rows_a[0:1, k * P:(k + 1) * P], end_cols[:, 0, k:k + 1], ident[:, :],
                          start=True, stop=True).then_inc(pre.ends_turned, 1)
            for k in range(NB):
                pe.matmul(rows_b[0:1, k * P:(k + 1) * P], end_cols[:, 1, k:k + 1], ident[:, :],
                          start=True, stop=True).then_inc(pre.ends_turned, 1)
            pe.wait_ge(pre.masks_ready, 1)
            mean_tensor(1)
            banks_left(1)

            pe.sem_inc(n2.gelu, FREE)
            with pe.Fori(0, NTG) as i:
                turn_two(n2, i, n2.rows)
                two_products(n2, i, n2.gelu, w_r[:, :], w_l[:, :], bias_row[:, :])
            for k, sums in enumerate((xc, xn)):
                pe.wait_ge(n2.gathered_sums, k + 1)
                for t in range(TG):
                    mm = pe.matmul(bank[:, 6 + k, 0:D], ones[:, :], sums[:, t, :], start=t == 0, stop=t == TG - 1)
                mm.then_inc(n2.colsum, 1)

            def table_turn(ready, base, k, i):
                pe.wait_ge(ready, base + i + 1)
                if not (isinstance(i, int) and i == 0):
                    pe.wait_ge(tab.copied, k * NTG + i)
                    pe.sem_inc(pe_tick, 1)
                for t in range(TG):
                    mm = pe.transpose(cols(0, t), xn[:, t, :], ident[:, :])
                mm.then_inc(tab.turned, 1)

            def table_product(k, i, n):
                pe.wait_ge(tab.copied, k * NTG + i + 1)
                pe.wait_ge(tab.rows, k * NTG + i + FREE)
                pe.wait_ge(tab.parts, k * NTG + i + FREE)
                for t in range(TG):
                    pe.matmul(cols(2, t), tr_a[:, t, :], w_att[:, n, 0:D], start=True, stop=True)
                for t in range(TG):
                    mm = pe.matmul(bank[:, 4, t * 2 * HEADS:(t + 1) * 2 * HEADS], tr_a[:, t, :],
                                   w_att[:, n, D:D + 2 * HEADS], start=True, stop=True)
                mm.then_inc(tab.product, 1)

            def table_rows(ready, base, k, n):
                table_turn(ready, base, k, 0)
                with pe.Fori(0, NTG - 1) as i:
                    table_turn(ready, base, k, i + 1)
                    table_product(k, i, n)
                table_product(k, NTG - 1, n)

            pe.sem_inc(tab.rows, FREE)
            pe.sem_inc(tab.parts, FREE)
            table_rows(ln.normed, 2 * NTG + FREE, 0, 0)

            for n in range(LAYERS):
                def score_quarter(j, slot):
                    _, at = nc.values_load_multi_w_load_instructions(
                        offsets[32:33, bass.ds(slot + 4 * j, 4)], engines=[PE_E], min_val=0,
                        max_val=(NT - 1) * PARTS * HEADS, skip_runtime_bounds_check_because=BOUNDED)
                    for k in range(4 * j, 4 * j + 4):
                        mm = pe.matmul(bank[:, 2, k * PARTS * HEADS:(k + 1) * PARTS * HEADS], pick_t[:, k, :],
                                       dst_parts[:, bass.ds(at[k % 4], PARTS * HEADS)], start=True, stop=True)
                    if j == QG - 1:
                        mm.then_inc(att.dst_scored, 1)

                if n == 0:
                    pe.sem_inc(att.added, FREE_BANKS)
                pe.wait_ge(att.turned, n * 2 * (NG + 1) + 2)
                for j in range(QG):
                    score_quarter(j, 0)
                with pe.Fori(0, PAIRS) as it:
                    for b in range(2):
                        done = n * NG + it * 2 + b
                        pe.wait_ge(att.scored, done + 1)
                        for h in range(HEADS):
                            mm = pe.transpose(bank[0:GROUP, 3, h * P:(h + 1) * P], score[:, h, :], ident[:, :])
                        mm.then_inc(att.score_rows, 1)
                        pe.wait_ge(att.firsts, done + 1)
                        pe.sem_inc(pe_tick, 1)
                        pe.transpose(bank[0:HEADS, 5, 0:GROUP], seg_f[:, P - 1::P],
                                     ident[0:GROUP, 0:GROUP])
                        pe.transpose(bank[0:HEADS, 5, GROUP:2 * GROUP], seg_m[:, 0::P],
                                     ident[0:GROUP, 0:GROUP]).then_inc(att.ends, 1)
                        pe.wait_ge(att.crossed, done + 1)
                        pe.sem_inc(pe_tick, 1)
                        pe.transpose(bank[0:GROUP, 5, 64:64 + HEADS], cross[:, 0, :], ident[0:HEADS, 0:HEADS])
                        pe.transpose(bank[0:GROUP, 5, 68:68 + HEADS], cross[:, 1, :],
                                     ident[0:HEADS, 0:HEADS]).then_inc(att.cross_rows, 1)
                        pe.wait_ge(att.maxima, done + 1)
                        pe.sem_inc(pe_tick, 1)
                        for h in range(HEADS):
                            mm = pe.transpose(bank[:, 4, h * GROUP:(h + 1) * GROUP],
                                              seg_m[:, h * P:(h + 1) * P], ident[0:GROUP, 0:GROUP])
                        mm.then_inc(att.max_back, 1)
                        picks = n * (NG + 1) * RNG + it * (2 * RNG) + b * RNG
                        pe.wait_ge(att.picked, picks + 1)
                        pe.wait_ge(att.log_scale, done + 1)
                        pe.matmul(bank[:, 5, 128:128 + HEADS], pick[0:1, 0, :], log_scale[:, :],
                                  start=True, stop=True).then_inc(att.scale_rows, 1)
                        for k in range(GROUP):
                            first = n * NS + it * (2 * GROUP) + b * GROUP
                            if k % ROUND == 0:
                                pe.wait_ge(att.picked, picks + k // ROUND + 1)
                            pe.wait_ge(att.weighted, first + k + 1)
                            pe.wait_ge(att.added, first + k + 1)
                            pe.matmul(bank[:, 4 + k % 4, 0:ROW], pick[:, k, :], gathered[:, b * GROUP + k, :],
                                      start=True, stop=True).then_inc(att.summed, 1)
                            if k == 3:
                                pe.wait_ge(att.turned, n * 2 * (NG + 1) + it * 4 + 2 * (b + 2))
                            if k % 4 == 3:
                                score_quarter(k // 4, it * (2 * GROUP) + (b + 1) * GROUP)
                if n < LAYERS - 1:
                    table_rows(n3.elu, n * NTG + FREE, n + 1, n + 1)
            pe.sem_inc(n3.added, FREE)
            with pe.Fori(0, NTG) as i:
                pe.wait_ge(n3.next, i + 1)
                pe.sem_inc(pe_tick, 1)
                for t in range(TG):
                    mm = pe.transpose(cols(4, t)[0:EA, :], cat[:, t, 2 * EA:3 * EA], ident[:, :])
                mm.then_inc(n3.turned, 1)
                pe.wait_ge(n3.added, i + FREE)
                pe.sem_inc(pe_tick, 1)
                for t in range(TG):
                    mm = pe.transpose(cols(2, t)[0:2 * EA, :], cat[:, t, 0:2 * EA], ident[:, :])
                mm.then_inc(n3.turned, 1)
                pe.wait_ge(ln.normed, 3 * NTG + i + 1 + FREE)
                for t in range(TG):
                    mm = pe.transpose(cols(0, t), xn[:, t, :], ident[:, :])
                mm.then_inc(n3.turned, 1)
                pe.wait_ge(n3.copied, i + 1)
                half = TG * P // 2
                for m in range(2):
                    for c in range(2):
                        for part_no, (rows, tr) in enumerate(((P, tr_a), (2 * EA, tr_b), (EA, tr_c))):
                            mm = pe.matmul(bank[:, 6 * (1 - m) + c, 0:half],
                                           w1[0:rows, part_no, m * P:(m + 1) * P],
                                           tr[0:rows, :, :].rearrange("p t n -> p (t n)")[:, c * half:(c + 1) * half],
                                           start=(part_no == 0), stop=(part_no == 2))
                    mm.then_inc(n3.hidden, 1)
                pe.wait_ge(n3.relu, 2 * i + 2)
                for t in range(TG):
                    for m in range(2):
                        mm = pe.matmul(cols(2, t), hid[:, m, t * P:(t + 1) * P], w2[:, m, :],
                                       start=(m == 0), stop=(m == 1))
                mm.then_inc(n3.product, 1)

        @block.vector
        def _(dve):
            def then():
                dve.drain()

            dve.wait_ge(pre.iota, 4)
            dve.tensor_copy(col_index[:, :], iota_i[:, :])
            dve.tensor_copy(part_index[:, :], iota_s[:, 0:1])
            dve.tensor_copy(slot_no, iota_s[:, 1:1 + NB])
            dve.memset(ones[:, :], 1.0)
            then()
            dve.tensor_scalar(ident[:, :], col_index[:, :], part_index[:, 0:1], None, ALU.is_equal)
            dve.tensor_scalar(tri_strict[:, :], col_index[:, :], part_index[:, 0:1], None, ALU.is_gt)
            dve.tensor_scalar(tri[:, :], col_index[:, :], part_index[:, 0:1], None, ALU.is_ge)
            dve.wait_ge(pre.tables_loaded, 32)
            dve.tensor_scalar(int_tmp[:, :, :], edge_now[:, :, 0::P - 1], 7, None, ALU.arith_shift_right)
            then()
            dve.tensor_copy(chunk_tile, int_tmp[:, :, 0])
            dve.tensor_copy(chunk_last, int_tmp[:, :, 1])
            then()
            dve.tensor_tensor(count, chunk_last, chunk_tile, ALU.subtract)
            then()
            dve.tensor_scalar(count, count, 1.0, None, ALU.add).then_inc(pre.counted, 1)
            dve.tensor_tensor(edge_cmp, edge_now, edge_before, ALU.is_equal)
            then()
            dve.tensor_copy(flag_b, edge_cmp)
            then()
            dve.tensor_scalar(flag_a, flag_b, 1.0, -EDGE_FAR, ALU.subtract, ALU.mult).then_inc(pre.edge_flags, 1)
            dve.wait_ge(pre.prefixed, 1)
            dve.tensor_copy(before, bank[:, 0, 0:NB])
            dve.tensor_copy(total, bank[:, 1, 0:NB])
            then()
            dve.tensor_tensor_scan(upto, ones[:, 0:NB], total, 0.0, ALU.mult, ALU.add)
            then()
            dve.tensor_tensor(before, before, upto, ALU.add)
            then()
            dve.tensor_tensor(before, before, total, ALU.subtract).then_inc(pre.placed, 1)
            then()
            dve.tensor_tensor(diag, ident[:, :].unsqueeze(1).to_broadcast([P, NB, P]),
                              before.unsqueeze(2).to_broadcast([P, NB, P]), ALU.mult).then_inc(pre.placed, 1)
            dve.wait_ge(pre.spread, NB)
            dve.tensor_copy(first_row, rows_b[:, 0:NR])
            then()
            for k in range(NB):
                dve.tensor_scalar(scratch, first_row, slot_no[:, k:k + 1], 0.0, ALU.is_le, ALU.add,
                                  accum_out=slots_to[:, k:k + 1])
                then()
            dve.tensor_scalar(chunk_of, slots_to, 1.0, None, ALU.subtract)
            then()
            dve.tensor_copy(chunk_idx[:, :], chunk_of).then_inc(pre.indexed, 1)

            def norm_var(i):
                for t in range(TG):
                    dve.bn_stats(ln_stats[:, t, :], x_flat[:, bass.ds(i * (TG * D) + t * D, D)])
                then()
                for t in range(TG):
                    dve.bn_aggr(ln_mean_var[:, t, :], ln_stats[:, t, :])
                then()
                dve.tensor_scalar(ln_root[:, 0, :], ln_mean_var[:, :, 1], EPS, None, ALU.add).then_inc(ln.var, 1)

            def norm_coef(i, base):
                dve.wait_ge(ln.normed, base + i + FREE)
                dve.wait_ge(ln.root, base + i + 1)
                dve.reciprocal(ln_coef[:, 0, :], ln_root[:, 1, :])
                then()
                dve.scalar_tensor_tensor(out=ln_coef[:, 1, :], in0=ln_mean_var[:, :, 0], scalar=-1.0,
                                         in1=ln_coef[:, 0, :], op0=ALU.mult, op1=ALU.mult).then_inc(ln.coef, 1)

            dve.memset(H[:, :, D:ROW], 1.0)
            dve.sem_inc(ln.normed, FREE)
            dve.wait_ge(pre.x_loaded, 16)
            with dve.Fori(0, NTG) as i:
                norm_var(i)
                norm_coef(i, 0)
            then()

            dve.wait_ge(pre.rows_gathered, 16 * NB)
            dve.wait_ge(pre.firsts_gathered, 16 * NB)
            dve.tensor_copy(src_row, sd_row[:, :, 0:P])
            dve.tensor_copy(dst_row, sd_row[:, :, P:2 * P + 1])
            dve.tensor_scalar(int_tmp[:, :, 0], sd_row[:, :, P], 7, None, ALU.arith_shift_right)
            then()
            dve.tensor_copy(tile_of, int_tmp[:, :, 0])
            dve.tensor_tensor(tmp, slot_no, first_of, ALU.subtract)
            dve.tensor_copy(end_cols[:, 0, :], dst_row[:, :, 0])
            dve.tensor_copy(end_cols[:, 1, :], dst_row[:, :, P - 1])
            dve.tensor_tensor(is_last, dst_row[:, :, 0:P], dst_row[:, :, 1:P + 1], ALU.not_equal)
            then()
            dve.tensor_tensor(tile_of, tile_of, tmp, ALU.add)
            dve.memset(change[:, :, 0:1], FAR)
            dve.memset(change[:, :, P:P + 1], FAR)
            dve.tensor_scalar(change[:, :, 1:P], is_last[:, :, 0:P - 1], FAR, None, ALU.mult)
            then()
            dve.tensor_scalar(tmp, tile_of, float(P), None, ALU.mult)
            dve.wait_ge(pre.flags_stored, 32)
            dve.tensor_copy(change_keep, change).then_inc(pre.changes, 1)
            dve.tensor_scalar(tile_of, tile_of, float(NT - 1), None, ALU.min)
            then()
            dve.tensor_tensor(dst_row[:, :, 0:P], dst_row[:, :, 0:P], tmp.unsqueeze(2).to_broadcast([P, NB, P]),
                              ALU.subtract)
            dve.memset(tile_cols[:, :, :], 0.0)
            dve.memset(dst_tail, -1.0)
            then()
            dve.tensor_copy(tile_cols[:, :, 0], tile_of)
            dve.tensor_copy(tile_cols[:, :, 32], tile_of).then_inc(pre.split, 1)
            dve.tensor_copy(dst_bf, dst_row[:, :, 0:P]).then_inc(pre.dst_kept, 1)
            dve.memset(dst_local[:, NR:], -1.0)
            dve.memset(src_of[:, NR:], 0.0)
            dve.memset(last_edge[:, NR:], 0.0)
            dve.memset(offsets[:, :], 0).then_inc(pre.tail_zeroed, 1)
            then()
            dve.wait_ge(pre.turned_b, 2 * NB)
            dve.tensor_copy(last_edge[:, 0:NR], rows_a[:, 0:NR]).then_inc(pre.copied_b, 1)
            dve.tensor_scalar(offsets[0:1, 0:NR], rows_b[0:1, 0:NR], float(ROW), None, ALU.mult)
            dve.tensor_scalar(offsets[32:33, 0:NR], rows_b[32:33, 0:NR], float(PARTS * HEADS), None, ALU.mult
                              ).then_inc(pre.copied_b, 1)
            dve.wait_ge(pre.w_turned, LAYERS)
            dve.tensor_copy(pick[:, 24:24 + LAYERS, :], bank[:, 0:LAYERS, 0:P]).then_inc(pre.w_copied, 1)
            dve.wait_ge(pre.w_made, LAYERS + 2)
            dve.tensor_copy(w_att[:, :, D:D + 2 * HEADS], bank[:, 4:4 + LAYERS, 0:2 * HEADS])
            dve.tensor_tensor(b1[:, :], b1[:, :], bank[:, 7, 0:2], ALU.add).then_inc(pre.w_kept, 1)
            dve.memset(minus_one[:, :], -1.0)

            dve.wait_ge(pre.changes_stored, 16)
            dve.wait_ge(pre.dst_stored, 32)
            then()
            dve.memset(acc[:, :], 0.0)
            dve.memset(ea_scan, 0.0)
            then()

            def build_picks(where, slot):
                return dve.tensor_tensor(pick[:, where:where + ROUND, :],
                                         dst_local[:, bass.ds(slot, ROUND)].unsqueeze(2).to_broadcast([P, ROUND, P]),
                                         col_index[:, :].unsqueeze(1).to_broadcast([P, ROUND, P]), ALU.is_equal)

            def add_sums(s, slot, base, k0, width):
                for k in range(k0, k0 + ROUND):
                    if k % 4 == 0:
                        _, at = nc.values_load_multi_w_load_instructions(
                            offsets[0:1, bass.ds(slot + k, 4)], engines=[DVE_E], min_val=0, max_val=(NT - 1) * ROW,
                            skip_runtime_bounds_check_because=BOUNDED)
                    row = acc[:, bass.ds(at[k % 4], width)]
                    dve.wait_ge(s.summed, base + k + 1)
                    dve.tensor_tensor(row, row, bank[:, 4 + k % 4, 0:width], ALU.add).then_inc(s.added, 1)
                    then()

            def add_sum(slot, summed, added, k):
                if k % 4 == 0:
                    _, at = nc.values_load_multi_w_load_instructions(
                        offsets[0:1, bass.ds(slot + k, 4)], engines=[DVE_E], min_val=0, max_val=(NT - 1) * ROW,
                        skip_runtime_bounds_check_because=BOUNDED)
                    tile_at[:] = at
                row = acc[:, bass.ds(tile_at[k % 4], ROW)]
                dve.wait_ge(att.added, added + k)
                dve.wait_ge(att.summed, summed + k + 1)
                dve.tensor_tensor(row, row, bank[:, 4 + k % 4, 0:ROW], ALU.add).then_inc(att.added, 1)

            tile_at = [None] * 4

            def mean_vector(n):
                if n == 0:
                    dve.sem_inc(mean.turned_back, FREE)
                with dve.Fori(0, NG) as it:
                    for q in range(RNG):
                        r = n * ROUNDS + q
                        build_picks(q * ROUND, it * GROUP + q * ROUND).then_inc(mean.picked, 1)
                        dve.wait_ge(mean.turned, it * RNG + r + 1)
                        dve.wait_ge(mean.turned_back, it * RNG + r + FREE)
                        for c in range(2):
                            scan = dve.tensor_tensor_scan(
                                ea_scan[:, c * 512:(c + 1) * 512], ea_flag[:, q % 2, c * 512:(c + 1) * 512],
                                bank[0:EA, c, :], ea_scan[:, 1023 - 512 * c:1024 - 512 * c],
                                ALU.add if n == 0 else ALU.mult, ALU.max if n == 0 else ALU.add)
                            if c == 0:
                                then()
                        scan.then_inc(mean.scanned, 1)
                        add_sums(mean, it * GROUP, n * NS + it * GROUP + FREE, q * ROUND, MEAN_W)

            def stores_landed(n):
                for b in range(2):
                    dve.wait_ge(mean_stored[b], 16 * ((n + 1) * (ROUNDS // 2) + FREE))
                dve.wait_ge(mean.turned_back, (n + 1) * ROUNDS + FREE)

            mean_vector(0)
            stores_landed(0)
            dve.tensor_copy(degree, acc_t[:, :, D]).then_inc(n1.degrees, 1)
            then()
            dve.tensor_scalar(inv_degree, degree, 1.0, None, ALU.max)
            dve.tensor_scalar(has_edge, degree, 1.0, None, ALU.min)
            then()
            dve.reciprocal(inv_degree, inv_degree).then_inc(n1.inverted, 1)
            with dve.Fori(0, NTG) as i:
                dve.wait_ge(n1.joined, i + 1)
                dve.wait_ge(n1.product, i + 1)
                x_group = X[:, bass.ds(i * TG, TG), :]
                dve.tensor_tensor(x_group, x_group, by_tile(flat(4)), ALU.add).then_inc(n1.taken, 1)
                then()
                norm_var(i)
                norm_coef(i, NTG)
            dve.tensor_scalar(no_edge_far, has_edge, 1.0, -FAR, ALU.subtract, ALU.mult)
            dve.tensor_copy(real_node, bank[:, 7, 64:64 + NT])
            then()
            dve.tensor_tensor_scan(rows_before, ones[:, 0:NT], real_node, -1.0, ALU.mult, ALU.add)
            then()
            dve.tensor_tensor(rows_before, rows_before, real_node, ALU.subtract)
            then()
            dve.tensor_tensor(rows_before, rows_before, bank[:, 7, 0:NT], ALU.add).then_inc(n1.prefix_used, 1)
            then()
            dve.tensor_scalar(rows_before, rows_before, 0.0, None, ALU.max)
            dve.tensor_copy(real_node, iota_nodes[:, :])
            then()
            dve.tensor_copy(last_row[:, :], rows_before)
            dve.tensor_scalar(real_node, real_node, float(g.nodes), None, ALU.is_lt)
            dve.wait_ge(pre.ends_turned, 2 * NB)
            dve.memset(masks_row, FAR)
            dve.memset(line_a, 0.0)
            dve.memset(line_b, 0.0)
            then()
            dve.tensor_copy(line_c, rows_a[0:1, 0:NR])
            dve.tensor_copy(line_d, rows_b[0:1, 0:NR])
            then()
            dve.tensor_tensor(line_a[:, 1:NR], line_c[:, 1:NR], line_d[:, 0:NR - 1], ALU.is_equal)
            dve.tensor_tensor(line_b[:, 0:NR], line_c, line_d, ALU.is_equal)
            then()
            dve.tensor_tensor(line_c, line_a[:, 0:NR], line_b[:, 0:NR], ALU.mult)
            dve.tensor_tensor(line_d[:, 0:NR - 1], line_a[:, 1:NR], line_b[:, 0:NR - 1], ALU.mult)
            then()
            dve.tensor_scalar(masks_row[:, 0, 0:NR], line_a[:, 0:NR], 1.0, -FAR, ALU.subtract, ALU.mult)
            dve.tensor_scalar(masks_row[:, 1, 0:NR], line_c, 1.0, -FAR, ALU.subtract, ALU.mult)
            dve.tensor_scalar(masks_row[:, 2, 0:NR - 1], line_d[:, 0:NR - 1], 1.0, -FAR, ALU.subtract, ALU.mult
                              ).then_inc(pre.masks_ready, 1)
            dve.wait_ge(pre.masks_stored, 16)
            then()
            dve.memset(acc[:, :], 0.0)
            dve.memset(ea_scan, 0.0)
            then()
            mean_vector(1)
            stores_landed(1)

            def mask_padding():
                for t in range(g.nodes // P, NT):
                    done = dve.tensor_scalar(acc_t[:, t, 0:D], acc_t[:, t, 0:D], real_node[:, t:t + 1], None, ALU.mult)
                return done

            def keep_both(i):
                dve.wait_ge(n2.turned, 2 * i + 1 + FREE)
                dve.tensor_copy(tr_a[:, :, :], by_tile(flat(0))).then_inc(n2.copied, 1)
                dve.wait_ge(n2.turned, 2 * i + 2 + FREE)
                dve.tensor_copy(tr_b[:, :, :], by_tile(flat(2))).then_inc(n2.copied, 1)

            def next_rows(i):
                if not (isinstance(i, int) and i == 0):
                    dve.wait_ge(n2.turned, 2 * i - 1 + FREE)
                    dve.sem_inc(dve_tick, 1)
                dve.tensor_copy(xn[:, :, :], H[:, bass.ds(i * TG, TG), 0:D]).then_inc(n2.rows, 1)

            def sum_f(i):
                dve.wait_ge(n2.gelu, i + 1 + FREE)
                dve.sem_inc(dve_tick, 1)
                return dve.tensor_tensor(xc[:, :, :], xc[:, :, :], acc_t[:, bass.ds(i * TG, TG), 0:D], ALU.add)

            def sum_f_before_last(i):
                if not (isinstance(i, int) and i == NTG - 1):
                    sum_f(i)
                    then()

            dve.memset(xc[:, :, :], 0.0)
            over_groups(dve, ((keep_both, 1), (next_rows, 2), (sum_f_before_last, 0)))
            dve.wait_ge(n2.gelu, NTG + FREE)
            mask_padding()
            then()
            sum_f(NTG - 1).then_inc(n2.gathered_sums, 1)
            dve.wait_ge(n2.colsum, 1)
            dve.scalar_tensor_tensor(out=tr_b[:, 2, :], in0=bank[:, 6, 0:D], scalar=1.0 / g.nodes,
                                     in1=norm_par[:, 2, :], op0=ALU.mult, op1=ALU.mult)
            then()

            def centre(i):
                out_group = acc_t[:, bass.ds(i * TG, TG), 0:D]
                return dve.tensor_tensor(out_group, out_group, tr_b[:, 2, :].unsqueeze(1).to_broadcast([P, TG, D]),
                                         ALU.subtract)

            def sum_squares(i):
                dve.wait_ge(n2.squares, i + 1)
                return dve.tensor_tensor(xn[:, :, :], xn[:, :, :], tr_a[:, :, :], ALU.add)

            dve.wait_ge(n2.joined, NTG)
            dve.memset(xn[:, :, :], 0.0)
            if NTG > 1:
                centre(0).then_inc(n2.centred, 1)
            if NTG > 2:
                with dve.Fori(0, NTG - 2) as i:
                    centre(i + 1).then_inc(n2.centred, 1)
                    sum_squares(i).then_inc(n2.summed, 1)
                    then()
            centre(NTG - 1)
            then()
            mask_padding().then_inc(n2.centred, 1)
            for i in range(max(NTG - 2, 0), NTG):
                then()
                sums = sum_squares(i)
                sums.then_inc(n2.summed if i < NTG - 1 else n2.gathered_sums, 1)
            dve.wait_ge(n2.colsum, 2)
            dve.tensor_scalar(tr_b[:, 1, :], bank[:, 7, 0:D], 1.0 / g.nodes, EPS, ALU.mult, ALU.add
                              ).then_inc(n2.colvar, 1)
            dve.wait_ge(n2.colroot, 1)
            dve.reciprocal(tr_b[:, 1, :], tr_b[:, 3, :])
            then()
            dve.tensor_tensor(tr_b[:, 0, :], tr_b[:, 1, :], norm_par[:, 0, :], ALU.mult).then_inc(n2.norm_ready, 1)
            then()

            def table_parts(k, i):
                scores = bank[:, 4, 0:TG * 2 * HEADS].rearrange("p (t h) -> p t h", t=TG)
                dst_scores = scores[:, :, HEADS:2 * HEADS]
                dve.wait_ge(tab.product, k * NTG + i + 1)
                dve.sem_inc(dve_tick, 1)
                dve.tensor_copy(score_t[:, bass.ds(i * TG, TG), :], dst_scores)
                dve.tensor_copy(H[:, bass.ds(i * TG, TG), AW:ROW], scores[:, :, 0:HEADS])
                dve.tensor_copy(H[:, bass.ds(i * TG, TG), 0:AW].rearrange(
                    "p t (h c) -> p t h c", h=HEADS)[:, :, :, HC],
                    ones[:, 0:TG * HEADS].rearrange("p (t h) -> p t h", t=TG))
                dve.tensor_copy(rest[:, :, :], dst_scores)
                dve.tensor_copy(parts_t[:, bass.ds(i * TG, TG), 0, :], dst_scores).then_inc(tab.parts, 1)
                for part_no in range(1, PARTS):
                    then()
                    dve.tensor_tensor(rest[:, :, :], rest[:, :, :],
                                      parts_t[:, bass.ds(i * TG, TG), part_no - 1, :], ALU.subtract)
                    then()
                    done = dve.tensor_copy(parts_t[:, bass.ds(i * TG, TG), part_no, :], rest[:, :, :])
                then()

            def normed(i):
                dve.wait_ge(n2.x_done, i + 1)
                dve.sem_inc(dve_tick, 1)
                norm_var(i)

            over_groups(dve, ((normed, 2), (lambda i: norm_coef(i, 2 * NTG), 2), (lambda i: table_parts(0, i), 0)))
            dve.wait_ge(tab.rows, NTG + FREE)
            dve.memset(acc[:, :], 0.0)
            dve.memset(cross[:, :, :], 0.0)
            dve.memset(log_scale[:, :], 0.0)
            then()

            edp = bank[:, 2, 0:GROUP * PARTS * HEADS].rearrange("p (s m h) -> p h s m", m=PARTS, h=HEADS)
            back = bank[:, 4, 0:P].rearrange("p (h s) -> p h s", h=HEADS)
            grp = bank[0:GROUP, 3, :]

            for n in range(LAYERS):
                if n:
                    dve.memset(acc[:, :], 0.0)
                dve.memset(carry_f[:, :], FAR)
                dve.memset(carry_b[:, :], FAR)

                def build_pick_t(part_no):
                    ks = slice(part_no * GROUP // 2, (part_no + 1) * GROUP // 2)
                    dve.tensor_scalar(pick_t[:, ks, :], pick_t[:, ks, :], part_index[:, 0:1], None,
                                      ALU.is_equal).then_inc(att.turned, 1)

                dve.wait_ge(att.rows_loaded, 16 * (n * (NG + 1) + 1))
                for part_no in range(2):
                    build_pick_t(part_no)
                with dve.Fori(0, PAIRS) as it:
                    for b in range(2):
                        done = n * NG + it * 2 + b
                        slot = it * (2 * GROUP) + b * GROUP
                        rows = gathered[:, b * GROUP:(b + 1) * GROUP, :]
                        dve.wait_ge(att.dst_scored, n * (NG + 1) + it * 2 + b + 1)
                        dve.sem_inc(dve_tick, 1)
                        dve.tensor_reduce(raw[:, :, :], edp, AX.X, ALU.add)
                        then()
                        dve.wait_ge(att_gathered[n][b], 16 * GROUP + it * (16 * GROUP))
                        dve.sem_inc(dve_tick, 1)
                        dve.tensor_tensor(raw[:, :, :], raw[:, :, :], rows[:, :, AW:ROW].rearrange("p s h -> p h s"),
                                          ALU.add)
                        then()
                        dve.scalar_tensor_tensor(out=score[:, :, :], in0=raw[:, :, :], scalar=SLOPE,
                                                 in1=raw[:, :, :], op0=ALU.mult, op1=ALU.max
                                                 ).then_inc(att.scored, 1)
                        dve.wait_ge(att_flags[b], 48 * (n * PAIRS + 1) + it * 48)
                        dve.wait_ge(att.score_rows, done + 1)
                        dve.tensor_tensor_scan(seg_f, start_flag[:, b, :], grp, FAR, ALU.add, ALU.max)
                        then()
                        dve.tensor_tensor_scan(seg_m[:, ::-1], end_flag[:, b, ::-1], seg_f[:, ::-1], FAR,
                                               ALU.add, ALU.max).then_inc(att.firsts, 1)
                        dve.wait_ge(att.ends, done + 1)
                        dve.tensor_tensor_scan(carry_f[:, 1:GROUP + 1], masks[:, b, 1, 0:GROUP],
                                               bank[0:HEADS, 5, 0:GROUP], carry_f[:, 0:1], ALU.add, ALU.max)
                        dve.tensor_tensor_scan(carry_b[:, 0:GROUP][:, ::-1], masks[:, b, 2, 0:GROUP][:, ::-1],
                                               bank[0:HEADS, 5, GROUP:2 * GROUP][:, ::-1], FAR, ALU.add, ALU.max)
                        then()
                        dve.tensor_tensor(cross[:, 0, :], carry_f[:, 0:GROUP], masks[:, b, 0, 0:GROUP], ALU.add)
                        dve.tensor_tensor(cross[:, 1, :], carry_b[:, 1:GROUP + 1], masks[:, b, 0, 1:GROUP + 1],
                                          ALU.add).then_inc(att.crossed, 1)
                        dve.wait_ge(att.rows_loaded, 16 * (n * (NG + 1) + b + 2) + it * 32)
                        dve.wait_ge(att.dst_scored, n * (NG + 1) + it * 2 + b + 1)
                        build_pick_t(0)
                        then()
                        dve.tensor_copy(carry_f[:, 0:1], carry_f[:, GROUP:GROUP + 1])
                        dve.wait_ge(att.cross_rows, done + 1)
                        dve.tensor_copy(cross_rows[:, :], bank[0:GROUP, 5, 64:72])
                        dve.tensor_copy(grp_sb, grp)
                        then()
                        dve.tensor_tensor(grp_sb[:, 0::P], grp_sb[:, 0::P], cross_rows[:, 0:HEADS], ALU.max)
                        then()
                        dve.tensor_tensor(grp_sb[:, P - 1::P], grp_sb[:, P - 1::P], cross_rows[:, HEADS:2 * HEADS],
                                          ALU.max)
                        then()
                        dve.tensor_tensor_scan(seg_f, start_flag[:, b, :], grp_sb, FAR, ALU.add, ALU.max)
                        then()
                        dve.tensor_tensor_scan(seg_m[:, ::-1], end_flag[:, b, ::-1], seg_f[:, ::-1], FAR,
                                               ALU.add, ALU.max).then_inc(att.maxima, 1)
                        build_pick_t(1)
                        dve.wait_ge(att.max_back, done + 1)
                        dve.tensor_tensor(score[:, :, :], score[:, :, :], back, ALU.subtract
                                          ).then_inc(att.shifted, 1)
                        dve.tensor_tensor(log_scale[:, :], cross_rows[0:1, 0:HEADS], bank[0:1, 4, 0:P:GROUP],
                                          ALU.subtract).then_inc(att.log_scale, 1)
                        dve.tensor_tensor(rows[:, :, AW:ROW].rearrange("p s h -> p h s"), back,
                                          last_edge[:, bass.ds(slot, GROUP)].unsqueeze(1)
                                          .to_broadcast([P, HEADS, GROUP]), ALU.mult)
                        _, at = nc.values_load_multi_w_load_instructions(
                            offsets[0:1, bass.ds(slot, 1)], engines=[DVE_E], min_val=0, max_val=(NT - 1) * ROW,
                            skip_runtime_bounds_check_because=BOUNDED)
                        dve.wait_ge(att.scale, done + 1)
                        dve.wait_ge(att.added, FREE_BANKS + n * NS + slot)
                        first = acc[:, bass.ds(at[0], AW)].rearrange("p (h c) -> p h c", h=HEADS)
                        dve.tensor_tensor(first, first, old_scale[:, :].unsqueeze(2).to_broadcast([P, HEADS, HW]),
                                          ALU.mult).then_inc(att.used, 1)
                        dve.wait_ge(att.prob, done + 1)
                        for k in range(GROUP + LEAD):
                            if k < GROUP:
                                part_rows = rows[:, k, 0:AW].rearrange("p (h c) -> p h c", h=HEADS)
                                dve.tensor_tensor(part_rows, part_rows,
                                                  prob[:, :, k].unsqueeze(2).to_broadcast([P, HEADS, HW]),
                                                  ALU.mult).then_inc(att.weighted, 1)
                            if k == LEAD:
                                dve.wait_ge(att.used, done + 1 + FREE)
                                dve.sem_inc(dve_tick, 1)
                            if k >= LEAD:
                                add_sum(slot, 2 * GROUP + n * NS + slot, FREE_BANKS + n * NS + slot, k - LEAD)

                dve.wait_ge(att.added, FREE_BANKS + (n + 1) * NS)
                dve.wait_ge(att.dst_scored, (n + 1) * (NG + 1))
                def heads(v):
                    return v[:, :, 0:AW].rearrange("p t (h c) -> p t h c", h=HEADS)

                dve.tensor_tensor(att_w[:, 0, :, :], H[:, :, AW:ROW], score_t, ALU.add)
                dve.tensor_tensor(att_w[:, 2, :, :], acc_t[:, :, AW:ROW],
                                  no_edge_far.unsqueeze(2).to_broadcast([P, NT, HEADS]), ALU.add)
                then()
                dve.scalar_tensor_tensor(out=att_w[:, 3, :, :], in0=att_w[:, 0, :, :], scalar=SLOPE,
                                         in1=att_w[:, 0, :, :], op0=ALU.mult, op1=ALU.max)
                then()
                dve.tensor_tensor(att_w[:, 1, :, :], att_w[:, 2, :, :], att_w[:, 3, :, :], ALU.max)
                then()
                dve.tensor_tensor(att_w[:, 2:4, :, :], att_w[:, 2:4, :, :],
                                  att_w[:, 1, :, :].unsqueeze(1).to_broadcast([P, 2, NT, HEADS]),
                                  ALU.subtract).then_inc(n3.scored, 1)
                dve.wait_ge(n3.weights, n * (NTG + 1) + 1)
                dve.tensor_tensor(att_w[:, 0, :, :], att_w[:, 2, :, :], heads(acc_t)[:, :, :, HC], ALU.mult)
                then()
                dve.tensor_tensor(att_w[:, 0, :, :], att_w[:, 0, :, :], att_w[:, 3, :, :], ALU.add)
                then()
                dve.reciprocal(att_w[:, 1, :, :], att_w[:, 0, :, :])
                then()
                dve.tensor_tensor(att_w[:, 4:6, :, :], att_w[:, 2:4, :, :],
                                  att_w[:, 1, :, :].unsqueeze(1).to_broadcast([P, 2, NT, HEADS]),
                                  ALU.mult).then_inc(n3.weighed, 1)
                then()

                def weigh_sums(i):
                    sums = heads(acc_t[:, bass.ds(i * TG, TG), :])[:, :, :, 0:HC]
                    dve.tensor_tensor(sums, sums, att_w[:, 4, bass.ds(i * TG, TG), :].unsqueeze(3)
                                      .to_broadcast([P, TG, HEADS, HC]), ALU.mult)
                    if n == LAYERS - 1:
                        own = xc[:, :, :].rearrange("p t (h c) -> p t h c", h=HEADS)
                        dve.tensor_tensor(own, heads(H[:, bass.ds(i * TG, TG), :])[:, :, :, 0:HC],
                                          att_w[:, 5, bass.ds(i * TG, TG), :].unsqueeze(3)
                                          .to_broadcast([P, TG, HEADS, HC]), ALU.mult)
                        then()
                        dve.tensor_tensor(xc[:, :, :], xc[:, :, :],
                                          att_bias[:, n, :].unsqueeze(1).to_broadcast([P, TG, D]), ALU.add)
                    else:
                        dve.wait_ge(n3.own_ready, n * NTG + i + 1)
                        dve.sem_inc(dve_tick, 1)
                    then()
                    done = dve.tensor_tensor(H[:, bass.ds(i * TG, TG), 0:D].rearrange("p t (h c) -> p t h c", h=HEADS),
                                             sums, xc[:, :, :].rearrange("p t (h c) -> p t h c", h=HEADS), ALU.add)
                    done.then_inc(n3.summed, 1)

                def elu(i, out):
                    dve.wait_ge(n3.weights, n * (NTG + 1) + i + 2)
                    dve.sem_inc(dve_tick, 1)
                    return dve.scalar_tensor_tensor(out=out, in0=H[:, bass.ds(i * TG, TG), 0:D], scalar=0.0,
                                                    in1=sq[:, :, :], op0=ALU.max, op1=ALU.add)

                if n < LAYERS - 1:
                    def elu_next(i):
                        if not (isinstance(i, int) and i == 0):
                            dve.wait_ge(tab.turned, (n + 1) * NTG + i)
                        elu(i, xn[:, :, :]).then_inc(n3.elu, 1)

                    over_groups(dve, ((elu_next, 2), (weigh_sums, 3), (lambda i: table_parts(n + 1, i), 0)))
                    dve.wait_ge(tab.rows, (n + 2) * NTG + FREE)

            def mlp_rows(i):
                x_group = X[:, bass.ds(i * TG, TG), :]
                elu(i, xc[:, :, :]).then_inc(n3.elu, 1)
                then()
                dve.scalar_tensor_tensor(out=x_group, in0=xc[:, :, :], scalar=1.0, in1=x_group,
                                         op0=ALU.subtract, op1=ALU.add)
                then()
                norm_var(i)
                if isinstance(i, int) and i == 0:
                    dve.wait_ge(n3.stats_gathered, 16 * NT)
                else:
                    dve.wait_ge(n3.turned, 3 * i)
                    dve.sem_inc(dve_tick, 1)
                dve.tensor_tensor(cat[:, :, 0:2 * EA], node_stats_in[:, bass.ds(i * TG, TG), :],
                                  has_edge[:, bass.ds(i * TG, TG)].unsqueeze(2).to_broadcast([P, TG, 2 * EA]),
                                  ALU.mult)
                then()
                dve.tensor_tensor(cat[:, :, 2 * EA:3 * EA], cat[:, :, 0:EA],
                                  inv_degree[:, bass.ds(i * TG, TG)].unsqueeze(2).to_broadcast([P, TG, EA]),
                                  ALU.mult).then_inc(n3.next, 1)
                norm_coef(i, 3 * NTG)

            def join_rows(i):
                x_group = X[:, bass.ds(i * TG, TG), :]
                dve.wait_ge(ln.normed, 3 * NTG + i + 1 + FREE)
                dve.sem_inc(dve_tick, 1)
                dve.tensor_tensor(x_group, x_group, xn[:, :, :], ALU.add).then_inc(n3.joined, 1)
                then()
                dve.tensor_tensor(x_group, x_group, node_bias[:, 1, :].unsqueeze(1).to_broadcast([P, TG, D]), ALU.add)
                then()

            def mlp_out(i):
                x_group = X[:, bass.ds(i * TG, TG), :]
                dve.wait_ge(n3.product, i + 1)
                dve.tensor_tensor(x_group, x_group, by_tile(flat(2)), ALU.add).then_inc(n3.added, 1)
                then()

            over_groups(dve, ((join_rows, 0), (mlp_rows, 1), (weigh_sums, 2), (mlp_out, 0)))


_ARGS = ["x", "chunks", "dst_line", "edge_attr", "w_self", "w_neigh", "b_neigh", "w_l", "w_r", "b_l", "gn_weight",
         "gn_bias", "mean_scale", "w_att", "att_src", "att_dst", "att_bias", "u", "w1", "b1", "w2", "b2"]


def kernel(x, src, dst, edge_attr_48, L0_gnn_w_self, L0_gnn_w_neigh, L0_gnn_b_neigh, L1_gnn_Wl, L1_gnn_bl,
           L1_gnn_Wr, L1_gnn_gn_weight, L1_gnn_gn_bias, L1_gnn_mean_scale, L2_gnn_W, L2_gnn_att_src,
           L2_gnn_att_dst, L2_gnn_bias, L3_gnn_u, L3_gnn_W1, L3_gnn_b1, L3_gnn_W2, L3_gnn_b2):
    import numpy as np
    import concourse.bacc as bacc
    from concourse.bass_utils import run_bass_kernel_spmd

    g = geometry(x.shape[0], src.shape[0])

    def padded(v, length, value):
        v = np.asarray(v)
        return np.concatenate([v, np.full((length - v.shape[0],) + v.shape[1:], value, v.dtype)])

    pad_node = g.tiles * P - 1
    src_p, dst_p = padded(src, g.rows * P, 0), padded(dst, g.rows * P, pad_node)
    chunks = np.zeros((g.rows, SD_W), np.int32)
    chunks[:, 0:P] = src_p.reshape(-1, P)
    chunks[:, P:2 * P] = dst_p.reshape(-1, P)
    chunks[:, 2 * P] = np.append(dst_p[P::P], np.int32(-1))
    arrays = {
        "x": padded(x, g.tiles * P, 0), "chunks": chunks,
        "dst_line": np.concatenate([np.full(1, -1, np.int32), dst_p]),
        "edge_attr": padded(edge_attr_48, g.rows * P, 0),
        "w_self": L0_gnn_w_self, "w_neigh": L0_gnn_w_neigh, "b_neigh": L0_gnn_b_neigh,
        "w_l": np.asarray(L1_gnn_Wl).T, "w_r": np.asarray(L1_gnn_Wr).T, "b_l": L1_gnn_bl,
        "gn_weight": L1_gnn_gn_weight, "gn_bias": L1_gnn_gn_bias, "mean_scale": L1_gnn_mean_scale,
        "w_att": L2_gnn_W, "att_src": L2_gnn_att_src, "att_dst": L2_gnn_att_dst, "att_bias": L2_gnn_bias,
        "u": L3_gnn_u, "w1": L3_gnn_W1, "b1": L3_gnn_b1, "w2": L3_gnn_W2, "b2": L3_gnn_b2,
    }
    nc = bacc.Bacc("TRN2", target_bir_lowering=False, num_devices=1)
    feeds, aps = {}, {}
    for name in _ARGS:
        v = np.ascontiguousarray(arrays[name])
        feeds[f"in_{name}"] = v
        aps[name] = nc.dram_tensor(f"in_{name}", v.shape, mybir.dt.from_np(v.dtype), kind="ExternalInput").ap()
    out = nc.dram_tensor("out_x", (g.tiles * P, D), F32, kind="ExternalOutput").ap()
    build_graph_network(nc, g, aps, out)
    r = run_bass_kernel_spmd(nc, [feeds], core_ids=[0])
    return r.results[0]["out_x"][:g.nodes]
```
